# Optimizing a Trainium2 kernel written in Bass

```python
import numpy as np
import jax
import jax.numpy as jnp

def _softmax(x, axis=-1):
    return jax.nn.softmax(x, axis=axis)

def _gelu(x):
    return jax.nn.gelu(x, approximate=True)

def _silu(x):
    return jax.nn.silu(x)

def _sigmoid(x):
    return jax.nn.sigmoid(x)

def _layernorm(x, axis=-1, eps=1e-05):
    m = jnp.mean(x, axis=axis, keepdims=True)
    v = jnp.var(x, axis=axis, keepdims=True)
    return (x - m) / jnp.sqrt(v + eps)

def _scatter_add(tgt, idx, src, axis=0):
    return tgt.at[idx].add(src)

def _segment_sum(src, seg, n):
    return jax.ops.segment_sum(src, seg, n)
kernel_name = 'mk_gnn_resnorm_d1_gnn_r32_2a2f4e'

def setup_inputs(seed: int=0):
    np.random.seed(seed)
    _w = jnp.asarray

    def _rec_inputs():
        import jax
        import jax.numpy as jnp
        _gk = jax.random.key(seed)
        x = -0.000202 + 1 * jax.random.normal(jax.random.fold_in(_gk, 1), (50000, 64), jnp.float32)
        _s = jax.random.randint(jax.random.fold_in(_gk, 2), (25000,), 0, 50000, jnp.int32)
        _d = jax.random.randint(jax.random.fold_in(_gk, 3), (25000,), 0, 50000, jnp.int32)
        _loop = jnp.arange(50000, dtype=jnp.int32)
        src = jnp.concatenate([_s, _d, _loop])
        dst = jnp.concatenate([_d, _s, _loop])
        _o = jnp.argsort(dst, stable=True)
        src = src[_o]
        dst = dst[_o]
        return (x, src, dst)
    x, src, dst = _rec_inputs()

    def _L0_gnn_setup():
        import jax, jax.numpy as jnp
        import numpy as np
        N_NODES = 3125
        N_EDGES = 50000
        D = 64

        def _ngcf_conv(x, W1, W2, src, dst, n_nodes):
            ones = jnp.ones(src.shape[0], dtype=x.dtype)
            deg_out = jnp.clip(jax.ops.segment_sum(ones, src, num_segments=n_nodes), 1.0)
            deg_in = jnp.clip(jax.ops.segment_sum(ones, dst, num_segments=n_nodes), 1.0)
            norm = jax.lax.rsqrt(deg_out[src] * deg_in[dst])
            h_src = x[src]
            h_dst = x[dst]
            msg = (h_src @ W1 + h_src * h_dst @ W2) * norm[:, None]
            agg = jax.ops.segment_sum(msg, dst, num_segments=n_nodes)
            return x @ W1 + agg
        key = jax.random.key(seed)
        ks = jax.random.split(key, 8)
        s = 1.0 / np.sqrt(D)
        return {'x': jax.random.normal(ks[0], (N_NODES, D), dtype=jnp.float32), 'edge_src': jax.random.randint(ks[1], (N_EDGES,), 0, N_NODES, dtype=jnp.int32), 'edge_dst': jax.random.randint(ks[2], (N_EDGES,), 0, N_NODES, dtype=jnp.int32), 'W1_1': jax.random.normal(ks[3], (D, D), dtype=jnp.float32) * s, 'W2_1': jax.random.normal(ks[4], (D, D), dtype=jnp.float32) * s, 'W1_2': jax.random.normal(ks[5], (D, D), dtype=jnp.float32) * s, 'W2_2': jax.random.normal(ks[6], (D, D), dtype=jnp.float32) * s}
    _L0_gnn_all = _L0_gnn_setup()
    _L0_gnn_in = {k: v for k, v in _L0_gnn_all.items() if k in ('W1_1', 'W2_1', 'W1_2', 'W2_2')}
    del _L0_gnn_all
    return {'x': x, 'src': src, 'dst': dst, 'L0_gnn_W1_1': _L0_gnn_in['W1_1'], 'L0_gnn_W2_1': _L0_gnn_in['W2_1'], 'L0_gnn_W1_2': _L0_gnn_in['W1_2'], 'L0_gnn_W2_2': _L0_gnn_in['W2_2']}

def reference(x, src, dst, L0_gnn_W1_1, L0_gnn_W2_1, L0_gnn_W1_2, L0_gnn_W2_2):
    import jax
    import jax.numpy as jnp

    def _L0_gnn_ref(x, edge_src, edge_dst, W1_1, W2_1, W1_2, W2_2):
        import jax, jax.numpy as jnp
        import numpy as np
        N_NODES = 3125
        N_EDGES = 50000
        D = 64

        def _ngcf_conv(x, W1, W2, src, dst, n_nodes):
            ones = jnp.ones(src.shape[0], dtype=x.dtype)
            deg_out = jnp.clip(jax.ops.segment_sum(ones, src, num_segments=n_nodes), 1.0)
            deg_in = jnp.clip(jax.ops.segment_sum(ones, dst, num_segments=n_nodes), 1.0)
            norm = jax.lax.rsqrt(deg_out[src] * deg_in[dst])
            h_src = x[src]
            h_dst = x[dst]
            msg = (h_src @ W1 + h_src * h_dst @ W2) * norm[:, None]
            agg = jax.ops.segment_sum(msg, dst, num_segments=n_nodes)
            return x @ W1 + agg
        n = x.shape[0]
        h = _ngcf_conv(x, W1_1, W2_1, edge_src, edge_dst, n)
        h = jax.nn.relu(h)
        h = _ngcf_conv(h, W1_2, W2_2, edge_src, edge_dst, n)
        return h
    x = _layernorm(x + _L0_gnn_ref(x, src, dst, L0_gnn_W1_1, L0_gnn_W2_1, L0_gnn_W1_2, L0_gnn_W2_2), axis=-1)
    return x

_drawn_inputs = setup_inputs


def setup_inputs(seed=0):
    import zlib

    import numpy as np

    out = dict(_drawn_inputs(seed))
    spreads = {}
    factors = {}
    for name, (base, spread) in spreads.items():
        noise = np.random.default_rng([zlib.crc32(name.encode()), seed]).standard_normal(out[name].shape)
        drawn = base * np.exp(spread * noise) if base else spread * noise
        out[name] = jnp.asarray(drawn.astype(out[name].dtype))
    for name, factor in factors.items():
        out[name] = (out[name] * factor).astype(out[name].dtype)
    return out
```

```python
from contextlib import ExitStack

import numpy as np

import concourse.bass as bass
from concourse import mybir

P = 128
N_NODES, D, N_EDGES = 50000, 64, 100000
EPS = 1e-5
F32 = mybir.dt.float32
I32 = mybir.dt.int32
ALU = mybir.AluOpType
ACT = mybir.ActivationFunctionType
AX = mybir.AxisListType

GP = 125
G_CHUNKS = N_EDGES // GP
G_TILES = N_NODES // GP
G_GROUP = 8
G_GROUPS = G_TILES // G_GROUP
assert G_CHUNKS * GP == N_EDGES and G_GROUPS * G_GROUP * GP == N_NODES
G_DRAM = {"g_table": (N_NODES, D), "g_hidden": (N_NODES, D), "g_sums": (N_NODES + GP, D),
          "g_deg0": (N_NODES + GP, 1), "g_deg1": (N_NODES + GP, 1)}


def general_path(nc, x, src, dst, weights, out, dram, run_if):
    with ExitStack() as ctx:
        def sb(name, shape, dt=F32):
            return ctx.enter_context(nc.sbuf_tensor("g_" + name, shape, dt))

        def sem(name):
            return ctx.enter_context(nc.semaphore("g_" + name))

        ident, before = sb("ident", [GP, GP]), sb("before", [GP, GP])
        spare_i, spare = sb("spare_i", [GP, 1], I32), sb("spare", [GP, 1])
        ones, zero, eps = sb("ones", [GP, 1]), sb("zero", [GP, G_GROUP * D]), sb("eps", [GP, 1])
        wcat = sb("wcat", [2 * D, 2, D])
        key_i, key, key_b = sb("key_i", [GP, 1], I32), sb("key", [GP, 1]), sb("key_b", [GP, GP])
        from_i = sb("from_i", [GP, 1], I32)
        same, same_before = sb("same", [GP, GP]), sb("same_before", [GP, GP])
        n_before, first, shifted, to_f = (sb(n, [GP, 1]) for n in ("n_before", "first", "shifted", "to_f"))
        to_i = sb("to_i", [GP, 1], I32)
        rows, total = sb("rows", [GP, D]), sb("total", [GP, D])
        deg, root, norm, newton = (sb(n, [GP, 2, G_TILES]) for n in ("deg", "root", "norm", "newton"))
        xg, sg, yg, zg, sq = (sb(n, [GP, G_GROUP, D]) for n in ("xg", "sg", "yg", "zg", "sq"))
        uv, uvt = sb("uv", [GP, G_GROUP, 2, D]), sb("uvt", [P, G_GROUP, GP])
        mean, var, std, rstd = (sb(n, [GP, G_GROUP]) for n in ("mean", "var", "std", "rstd"))
        res = sb("res", [GP, G_GROUP, D])
        p_row = ctx.enter_context(nc.psum_tensor("g_p_row", [GP, 512], F32))
        p_sum = ctx.enter_context(nc.psum_tensor("g_p_sum", [GP, 512], F32))
        p_turn = [ctx.enter_context(nc.psum_tensor(f"g_p_turn{h}", [P, 512], F32)) for h in range(2)]
        p_out = ctx.enter_context(nc.psum_tensor("g_p_out", [GP, 512], F32))

        made, consts, cleared, w_in = sem("made"), sem("consts"), sem("cleared"), sem("w_in")
        key_in, key_spread, key_turned, same_made = sem("key_in"), sem("key_spread"), sem("key_turned"), sem("same_made")
        gathered, summed, total_made, added = sem("gathered"), sem("summed"), sem("total_made"), sem("added")
        deg_in, deg_made, rooted = sem("deg_in"), sem("deg_made"), sem("rooted")
        group_in, sums_in, uv_made, turned, uvt_made = sem("group_in"), sem("sums_in"), sem("uv_made"), sem("turned"), sem("uvt_made")
        multiplied, act_made, centred, squared = sem("multiplied"), sem("act_made"), sem("centred"), sem("squared")
        var_made, std_made, group_made, group_out = sem("var_made"), sem("std_made"), sem("group_made"), sem("group_out")
        hidden_out = sem("hidden_out")
        block = ctx.enter_context(nc.Block())

        by_lane = "(p t) d -> p t d"
        xv, ov = x.rearrange(by_lane, p=GP), out.rearrange(by_lane, p=GP)
        tv, hv = dram["g_table"].rearrange(by_lane, p=GP), dram["g_hidden"].rearrange(by_lane, p=GP)
        sv = dram["g_sums"][0:N_NODES, :].rearrange(by_lane, p=GP)
        PASSES = [(src, dram["g_deg0"], False), (dst, dram["g_deg1"], False),
                  (dst, dram["g_sums"], True), (dst, dram["g_sums"], True)]

        @block.sync
        def _(sp):
            with run_if(sp):
                for l in range(2):
                    for k in range(2):
                        sp.dma_start(wcat[k * D:(k + 1) * D, l, :], weights[2 * l + k]).then_inc(w_in, 16)

                def keys(n):
                    with sp.Fori(0, G_CHUNKS) as c:
                        sp.dma_start(key_i[:, :], PASSES[n][0][bass.ds(c * GP, GP)].unsqueeze(1)).then_inc(key_in, 16)
                        sp.dma_start(from_i[:, :], src[bass.ds(c * GP, GP)].unsqueeze(1)).then_inc(key_in, 16)
                        sp.wait_ge(added, 16 * c + 16 * (1 + n * G_CHUNKS))
                        sp.nop(nofuse=True)

                part = lambda g: bass.ds(g * G_GROUP, G_GROUP)
                keys(0)
                keys(1)
                sp.wait_ge(added, 16 * 2 * G_CHUNKS)
                for k in range(2):
                    sp.dma_start(deg[:, k, :], dram[f"g_deg{k}"][0:N_NODES, :].rearrange("(p t) one -> p (t one)", p=GP)).then_inc(deg_in, 16)
                with sp.Fori(0, G_GROUPS) as g:
                    sp.dma_start(xg[:, :, :], xv[:, part(g), :]).then_inc(group_in, 16)
                    sp.wait_ge(group_made, g + 1)
                    sp.dma_start(tv[:, part(g), :], yg[:, :, :]).then_inc(group_out, 16)
                    sp.wait_ge(group_out, 16 * g + 16)
                    sp.nop(nofuse=True)
                for l in range(2):
                    keys(2 + l)
                    sp.wait_ge(added, 16 * (3 + l) * G_CHUNKS)
                    done = G_GROUPS * (1 + l)
                    with sp.Fori(0, G_GROUPS) as g:
                        sp.dma_start(xg[:, :, :], (xv if l == 0 else hv)[:, part(g), :]).then_inc(group_in, 16)
                        sp.dma_start(res[:, :, :], xv[:, part(g), :]).then_inc(group_in, 16)
                        sp.dma_start(sg[:, :, :], sv[:, part(g), :]).then_inc(group_in, 16)
                        sp.wait_ge(group_made, g + (1 + done))
                        sp.dma_start((tv if l == 0 else ov)[:, part(g), :], yg[:, :, :]).then_inc(group_out, 16)
                        if l == 0:
                            sp.dma_start(hv[:, part(g), :], zg[:, :, :]).then_inc(hidden_out, 16)
                            sp.wait_ge(hidden_out, 16 * g + 16)
                            sp.nop(nofuse=True)
                        sp.wait_ge(group_out, 16 * g + 16 * (1 + done))
                        sp.nop(nofuse=True)

        @block.gpsimd
        def _(pool):
            with run_if(pool):
                nc.gpsimd.memset(ident[:, :], 0.0).then_inc(consts, 1)
                nc.gpsimd.memset(before[:, :], 1.0).then_inc(consts, 1)
                nc.gpsimd.memset(zero[:, :], 0.0).then_inc(consts, 1)
                nc.gpsimd.iota(spare_i[:, :], pattern=[[1, 1]], base=N_NODES, channel_multiplier=1).then_inc(consts, 1)
                pool.wait_ge(consts, 4)
                nc.gpsimd.affine_select(out=ident[:, :], in_=ident[:, :], compare_op=ALU.not_equal, fill=1.0,
                                        base=0, pattern=[[-1, GP]], channel_multiplier=1).then_inc(consts, 1)
                nc.gpsimd.affine_select(out=before[:, :], in_=before[:, :], compare_op=ALU.is_gt, fill=0.0,
                                        base=0, pattern=[[-1, GP]], channel_multiplier=1).then_inc(consts, 1)

                def clear_sums():
                    with pool.Fori(0, G_GROUPS) as g:
                        pool.dma_start(sv[:, bass.ds(g * G_GROUP, G_GROUP), :],
                                       zero[:, :].rearrange("p (t d) -> p t d", d=D)).then_inc(cleared, 16)
                for k in range(2):
                    pool.dma_start(dram[f"g_deg{k}"][0:N_NODES, :].rearrange("(p t) one -> p (t one)", p=GP),
                                   zero[:, 0:G_TILES]).then_inc(cleared, 16)
                    pool.dma_start(dram[f"g_deg{k}"][N_NODES:, :], zero[:, 0:1]).then_inc(cleared, 16)
                clear_sums()
                pool.dma_start(dram["g_sums"][N_NODES:, :], zero[:, 0:D]).then_inc(cleared, 16)
                pool.wait_ge(cleared, 16 * (5 + G_GROUPS))
                for n, (_, into, gather) in enumerate(PASSES):
                    done = n * G_CHUNKS
                    if n == 3:
                        pool.wait_ge(group_in, 16 * 4 * G_GROUPS)
                        clear_sums()
                        pool.wait_ge(cleared, 16 * (5 + 2 * G_GROUPS))
                    with pool.Fori(0, G_CHUNKS) as c:
                        if gather:
                            pool.wait_ge(key_in, 32 * c + 32 * (1 + done))
                            pool.nop(nofuse=True)
                            pool.wait_ge(group_out, 16 * G_GROUPS * (n - 1))
                            pool.indirect_dma_start(out=rows[:, :], out_offset=None, in_=dram["g_table"],
                                                    in_offset=bass.IndirectOffsetOnAxis(ap=from_i[:, :], axis=0)).then_inc(gathered, 16)
                        pool.wait_ge(total_made, c + (1 + done))
                        pool.nop(nofuse=True)
                        pool.indirect_dma_start(out=into, out_offset=bass.IndirectOffsetOnAxis(ap=to_i[:, :], axis=0),
                                                in_=total[:, 0:D if gather else 1], in_offset=None, compute_op=ALU.add).then_inc(added, 16)
                        pool.wait_ge(added, 16 * c + 16 * (1 + done))
                        pool.nop(nofuse=True)

        @block.tensor
        def _(pe):
            with run_if(pe):
                pe.wait_ge(consts, 6)
                pe.wait_ge(w_in, 64)

                def edges(n):
                    done, gather = n * G_CHUNKS, PASSES[n][2]
                    with pe.Fori(0, G_CHUNKS) as c:
                        pe.wait_ge(key_spread, c + (1 + done))
                        nc.tensor.matmul(p_row[:, 0:GP], key_b[:, :], ident[:, :], start=True, stop=True).then_inc(key_turned, 1)
                        pe.wait_ge(same_made, c + (1 + done))
                        if gather:
                            pe.wait_ge(gathered, 16 * c + 16 * (1 + (n - 2) * G_CHUNKS))
                            nc.tensor.matmul(p_sum[:, 0:D], same[:, :], rows[:, :], start=True, stop=True).then_inc(summed, 1)
                        else:
                            nc.tensor.matmul(p_sum[:, 0:1], same[:, :], ones[:, :], start=True, stop=True).then_inc(summed, 1)
                edges(0)
                edges(1)
                for l in range(2):
                    edges(2 + l)
                    with pe.Fori(0, G_GROUPS) as g:
                        pe.wait_ge(uv_made, g + (1 + l * G_GROUPS))
                        for t in range(G_GROUP):
                            last = nc.tensor.transpose(p_turn[t // 4][:, (t % 4) * GP:(t % 4 + 1) * GP],
                                                       uv[:, t].rearrange("p a d -> p (a d)"), ident[:, :])
                        last.then_inc(turned, 1)
                        pe.wait_ge(uvt_made, g + (1 + l * G_GROUPS))
                        for t in range(G_GROUP):
                            last = nc.tensor.matmul(p_out[:, t * D:(t + 1) * D], uvt[:, t, :], wcat[:, l, :], start=True, stop=True)
                        last.then_inc(multiplied, 1)

        @block.scalar
        def _(act):
            with run_if(act):
                act.wait_ge(deg_made, 1)
                nc.scalar.activation(root[:, :, :], deg[:, :, :], ACT.Sqrt).then_inc(rooted, 1)
                for l in range(2):
                    with act.Fori(0, G_GROUPS) as g:
                        act.wait_ge(turned, g + (1 + l * G_GROUPS))
                        nc.scalar.activation(uvt[:, 0:4, :], p_turn[0][:, 0:4 * GP].rearrange("p (t n) -> p t n", n=GP), ACT.Copy)
                        nc.scalar.activation(uvt[:, 4:8, :], p_turn[1][:, 0:4 * GP].rearrange("p (t n) -> p t n", n=GP),
                                             ACT.Copy).then_inc(uvt_made, 1)
                        if l == 1:
                            act.wait_ge(centred, g + 1)
                            nc.scalar.activation(sq[:, :, :], zg[:, :, :], ACT.Square).then_inc(squared, 1)
                            act.wait_ge(var_made, g + 1)
                            nc.scalar.activation(std[:, :], var[:, :], ACT.Sqrt, bias=eps[:, :], scale=1.0 / D).then_inc(std_made, 1)

        @block.vector
        def _(dve):
            with run_if(dve):
                V = nc.vector
                V.memset(ones[:, :], 1.0)
                V.memset(eps[:, :], EPS)
                dve.wait_ge(consts, 6)
                V.tensor_copy(spare[:, :], spare_i[:, :]).then_inc(made, 1)
                dve.wait_ge(made, 1)
                count = [1]

                def stepper(base, per_round, i):
                    n = [0]

                    def step(ins):
                        n[0] += 1
                        ins.then_inc(made, 1)
                        dve.wait_ge(made, i * per_round + (base + n[0]))
                    return step, n

                def edges(n):
                    done, gather = n * G_CHUNKS, PASSES[n][2]
                    K = 8
                    with dve.Fori(0, G_CHUNKS) as c:
                        step, k = stepper(count[0], K, c)
                        dve.wait_ge(key_in, 32 * c + 32 * (1 + done))
                        step(V.tensor_copy(key[:, :], key_i[:, :]))
                        V.tensor_copy(key_b[:, :], key[:, :].to_broadcast([GP, GP])).then_inc(key_spread, 1)
                        step(V.tensor_tensor(shifted[:, :], key[:, :], spare[:, :], ALU.subtract))
                        dve.wait_ge(key_turned, c + (1 + done))
                        step(V.tensor_scalar(same[:, :], p_row[:, 0:GP], key[:, :], None, ALU.is_equal))
                        V.tensor_copy(total[:, 0:1], ones[:, :]).then_inc(same_made, 1)
                        step(V.tensor_tensor(same_before[:, :], same[:, :], before[:, :], ALU.mult))
                        step(V.tensor_reduce(n_before[:, :], same_before[:, :], AX.X, ALU.add))
                        step(V.tensor_scalar(first[:, :], n_before[:, :], 0.0, None, ALU.is_equal))
                        step(V.scalar_tensor_tensor(to_f[:, :], shifted[:, :], first[:, :], spare[:, :], ALU.mult, ALU.add))
                        step(V.tensor_copy(to_i[:, :], to_f[:, :]))
                        dve.wait_ge(summed, c + (1 + done))
                        w = D if gather else 1
                        V.tensor_copy(total[:, 0:w], p_sum[:, 0:w]).then_inc(total_made, 1)
                        assert k[0] == K
                    count[0] += K * G_CHUNKS

                def spread(k, g):
                    return norm[:, k, bass.ds(g * G_GROUP, G_GROUP)].unsqueeze(2).to_broadcast([GP, G_GROUP, D])
                edges(0)
                edges(1)
                dve.wait_ge(deg_in, 32)
                step, k = stepper(count[0], 0, 0)
                step(V.tensor_scalar(deg[:, :, :], deg[:, :, :], 1.0, None, ALU.max))
                V.memset(newton[:, :, :], 0.0).then_inc(deg_made, 1)
                dve.wait_ge(rooted, 1)
                step(V.reciprocal(norm[:, :, :], root[:, :, :]))
                step(V.tensor_tensor(newton[:, :, :], norm[:, :, :], norm[:, :, :], ALU.mult))
                step(V.tensor_tensor(newton[:, :, :], newton[:, :, :], deg[:, :, :], ALU.mult))
                step(V.tensor_scalar(newton[:, :, :], newton[:, :, :], -0.5, 1.5, ALU.mult, ALU.add))
                step(V.tensor_tensor(norm[:, :, :], norm[:, :, :], newton[:, :, :], ALU.mult))
                count[0] += k[0]
                with dve.Fori(0, G_GROUPS) as g:
                    dve.wait_ge(group_in, 16 * g + 16)
                    V.tensor_tensor(yg[:, :, :], xg[:, :, :], spread(0, g), ALU.mult).then_inc(group_made, 1)
                for l in range(2):
                    edges(2 + l)
                    K = 3 if l == 0 else 7
                    with dve.Fori(0, G_GROUPS) as g:
                        step, k = stepper(count[0], K, g)
                        dve.wait_ge(group_in, 48 * g + (48 + 16 * G_GROUPS + 48 * l * G_GROUPS))
                        step(V.tensor_tensor(sg[:, :, :], sg[:, :, :], spread(1, g), ALU.mult))
                        V.tensor_tensor(uv[:, :, 0, :], sg[:, :, :], xg[:, :, :], ALU.add)
                        step(V.tensor_tensor(uv[:, :, 1, :], sg[:, :, :], xg[:, :, :], ALU.mult))
                        V.tensor_copy(mean[:, :], norm[:, 0, 0:G_GROUP]).then_inc(uv_made, 1)
                        dve.wait_ge(multiplied, g + (1 + l * G_GROUPS))
                        product = p_out[:, 0:G_GROUP * D].rearrange("p (t d) -> p t d", d=D)
                        if l == 0:
                            step(V.tensor_scalar(zg[:, :, :], product, 0.0, None, ALU.max))
                            V.tensor_tensor(yg[:, :, :], zg[:, :, :], spread(0, g), ALU.mult).then_inc(group_made, 1)
                        else:
                            across = lambda a: a[:, :].unsqueeze(2).to_broadcast([GP, G_GROUP, D])
                            step(V.tensor_tensor(zg[:, :, :], res[:, :, :], product, ALU.add))
                            step(V.tensor_reduce(mean[:, :], zg[:, :, :], AX.X, ALU.add))
                            step(V.tensor_scalar(mean[:, :], mean[:, :], 1.0 / D, None, ALU.mult))
                            V.tensor_tensor(zg[:, :, :], zg[:, :, :], across(mean), ALU.subtract).then_inc(centred, 1)
                            dve.wait_ge(squared, g + 1)
                            step(V.tensor_reduce(var[:, :], sq[:, :, :], AX.X, ALU.add))
                            V.tensor_copy(mean[:, :], norm[:, 0, 0:G_GROUP]).then_inc(var_made, 1)
                            dve.wait_ge(std_made, g + 1)
                            step(V.reciprocal(rstd[:, :], std[:, :]))
                            V.tensor_tensor(yg[:, :, :], zg[:, :, :], across(rstd), ALU.mult).then_inc(group_made, 1)
                        assert k[0] == K
                    count[0] += K * G_GROUPS


INPUTS = ["x", "src", "dst", "L0_gnn_W1_1", "L0_gnn_W2_1", "L0_gnn_W1_2", "L0_gnn_W2_2"]


def kernel(**inputs):
    import concourse.bacc as bacc
    from concourse.bass_utils import run_bass_kernel_spmd
    from contextlib import nullcontext

    nc = bacc.Bacc("TRN2", target_bir_lowering=False, num_devices=1)
    arrays, aps = {}, {}
    for name in INPUTS:
        a = np.ascontiguousarray(inputs[name])
        arrays["in_" + name] = a
        aps[name] = nc.dram_tensor("in_" + name, a.shape, mybir.dt.from_np(a.dtype), kind="ExternalInput").ap()
    out = nc.dram_tensor("out", (N_NODES, D), F32, kind="ExternalOutput").ap()
    dram = {n: nc.dram_tensor(n, s, F32, kind="Internal").ap() for n, s in G_DRAM.items()}
    general_path(nc, aps["x"], aps["src"], aps["dst"], [aps[n] for n in INPUTS[3:]], out, dram, lambda e: nullcontext())
    r = run_bass_kernel_spmd(nc, [arrays], core_ids=[0])
    return r.results[0]["out"]
```

```python
from contextlib import ExitStack

import numpy as np

import concourse.bass as bass
from concourse import mybir

P = 128
N_NODES, D, N_EDGES = 50000, 64, 100000
EPS = 1e-5
F32 = mybir.dt.float32
I32 = mybir.dt.int32
ALU = mybir.AluOpType
ACT = mybir.ActivationFunctionType
AX = mybir.AxisListType

P = 128
GN = 8
GROUP_NODES = GN * P
GROUPS = -(-N_NODES // GROUP_NODES)
TILES = GROUPS * GN
FULL_TILES = N_NODES // P
LAST_ROWS = N_NODES - FULL_TILES * P
CG = GN + 1
CHUNKS = GROUPS * CG
GROUP_SLOTS = CG * P
EB = 7
RUN = EB * P
EP = -(-N_EDGES // RUN)
LAST_RUN = N_EDGES - (EP - 1) * RUN
RAWS = EP * EB
RG = RAWS // GROUPS
HALO = P
WIN = 9
BACK = 4
SPAN = RG // 2 - 1 + WIN
GRID = (GROUPS - 1) * CG + SPAN
NO_EDGE = 65536
FAR = 10000.0
CAP = 2000.0
REACH = [[t for t in (j - 1, j, j + 1) if 0 <= t < GN] for j in range(CG)]
WIDTH = [P * len(r) for r in REACH]
SKIP = [P * (r[0] - (j - 1)) for j, r in enumerate(REACH)]
START = [sum(WIDTH[:j]) for j in range(CG)]
F16 = mybir.dt.float16
assert GROUPS % 2 == 1 and RAWS == GROUPS * RG and RG % 2 == 0 and LAST_RUN > HALO and TILES - FULL_TILES == 2


def runs(e, first, last):
    return e[first * RUN:last * RUN].rearrange("(p j) -> p j", j=RUN)


def place_edges(nc, src, dst, keepers):
    k = keepers
    with ExitStack() as ctx:
        def sb(name, shape, dt=F32):
            return ctx.enter_context(nc.sbuf_tensor("a_" + name, shape, dt))

        def sem(name):
            return ctx.enter_context(nc.semaphore("a_" + name))

        W = HALO + RUN
        s_i, d_i = sb("s_i", [EP, W], I32), sb("d_i", [EP, W + 1], I32)
        sf, df = sb("sf", [EP, W]), sb("df", [EP, W + 1])
        number = sb("number", [EP, W])
        is_self, step_up, drop, drop_no, last_drop = (sb(n, [EP, W]) for n in ("is_self", "step_up", "drop", "drop_no", "last_drop"))
        group_i, group = sb("group_i", [EP, RUN + 1], I32), sb("group", [EP, RUN + 1])
        kept_before, starts, base, behind, slot, keep, dev, degree, m1, m2, col_s, col_n = (
            sb(n, [EP, RUN]) for n in ("kept_before", "starts", "base", "behind", "slot", "keep", "dev", "degree", "m1", "m2", "col_s", "col_n"))
        place_i, target_i, lane_i, col_i, high_i, low_i = (sb(n, [EP, RUN], I32) for n in ("place_i", "target_i", "lane_i", "col_i", "high_i", "low_i"))
        lane, high, low = (sb(n, [EP, RUN]) for n in ("lane", "high", "low"))
        base_row, carry_row, carry = sb("base_row", [1, EP]), sb("carry_row", [1, EP + 1]), sb("carry", [EP, 1])
        extreme = sb("extreme", [EP, 4])
        win_s, win_n = sb("win_s", [P, RAWS]), sb("win_n", [P, RAWS])
        bank = [ctx.enter_context(nc.psum_tensor(f"a_bank{i}", [P, 512], F32)) for i in range(8)]
        padded, edges_in, w_in, consts, selected = sem("padded"), sem("edges_in"), sem("w_in"), sem("consts"), sem("selected")
        made, ints_made, floats_made = sem("made"), sem("ints_made"), sem("floats_made")
        base_made, base_up, carry_made, carry_down = sem("base_made"), sem("base_up"), sem("carry_made"), sem("carry_down")
        arrays_made, turned, copied, columned = sem("arrays_made"), sem("turned"), sem("copied"), sem("columned")
        block = ctx.enter_context(nc.Block())

        OWN = slice(HALO, W)
        BEFORE = slice(HALO - 1, W - 1)
        by_raw = lambda a: a.rearrange("q (p b) -> q b p", b=EB)
        ARRAYS = [(col_s, None), (col_n, None), (lane, k.lane_r[:, :]), (degree, k.deg_r[:, :]),
                  (high, k.parts[:, :, 0]), (low, k.parts[:, :, 1]), (dev, k.parts[:, :, 2])]

        def halves(a):
            return [(bank[(2 * a + h) % 8], 4 * h, min(4, EB - 4 * h)) for h in range(2)]

        @block.sync
        def _(sp):
            for l in range(2):
                for j in range(2):
                    sp.dma_start(k.wcat[j * D:(j + 1) * D, l, :], k.weights[2 * l + j]).then_inc(w_in, 16)
            sp.wait_ge(padded, 1)
            for e, to in ((dst, d_i), (src, s_i)):
                sp.dma_start(to[0:EP - 1, OWN], runs(e, 0, EP - 1)).then_inc(edges_in, 16)
                sp.dma_start(to[EP - 1:EP, HALO:HALO + LAST_RUN], e[(EP - 1) * RUN:N_EDGES].unsqueeze(0)).then_inc(edges_in, 16)
                sp.dma_start(to[1:EP, 0:HALO], runs(e, 0, EP - 1)[:, RUN - HALO:RUN]).then_inc(edges_in, 16)
            sp.dma_start(d_i[0:EP - 2, W:W + 1], runs(dst, 1, EP - 1)[:, 0:1], allow_slow_non_contiguous=True).then_inc(edges_in, 16)
            sp.dma_start(d_i[EP - 2:EP - 1, W:W + 1], dst[(EP - 1) * RUN:(EP - 1) * RUN + 1].unsqueeze(0)).then_inc(edges_in, 16)
            sp.wait_ge(w_in, 64)

        @block.gpsimd
        def _(pool):
            G = nc.gpsimd
            free = dict(allow_small_or_imprecise_dtypes=True)
            G.memset(k.ident[:, :], 0.0).then_inc(selected, 1)
            G.iota(number[:, :], pattern=[[1, W]], base=1 - HALO, channel_multiplier=RUN, **free).then_inc(consts, 1)
            pool.wait_ge(selected, 1)
            G.affine_select(out=k.ident[:, :], in_=k.ident[:, :], compare_op=ALU.not_equal, fill=1.0,
                            base=0, pattern=[[-1, P]], channel_multiplier=1).then_inc(consts, 1)
            G.iota(win_s[:, :], pattern=[[CG, GROUPS], [1, RG // 2], [0, 2]], base=-BACK, channel_multiplier=0, **free).then_inc(consts, 1)
            G.iota(win_n[:, :], pattern=[[1, RAWS // 2], [0, 2]], base=-BACK, channel_multiplier=0, **free).then_inc(consts, 1)
            G.iota(k.place[:, :], pattern=[[1, 3 * P]], base=0, channel_multiplier=0, **free).then_inc(consts, 1)
            G.iota(k.place16[:, :], pattern=[[1, TILES]], base=0, channel_multiplier=0, **free).then_inc(consts, 1)
            G.iota(k.lane_no[:, :], pattern=[[1, 1]], base=0, channel_multiplier=1, **free).then_inc(consts, 1)

        @block.tensor
        def _(pe):
            pe.wait_ge(consts, 7)
            pe.wait_ge(base_made, 1)
            nc.tensor.transpose(bank[0][0:1, 0:EP], base[:, RUN - 1:RUN], k.ident[0:EP, 0:EP]).then_inc(base_up, 1)
            pe.wait_ge(carry_made, 1)
            nc.tensor.matmul(bank[1][0:EP, 0:1], carry_row[0:1, 0:EP], k.ones[0:1, 0:1], start=True, stop=True).then_inc(carry_down, 1)
            for a, (array, _) in enumerate(ARRAYS):
                if a == 0:
                    pe.wait_ge(arrays_made, 1)
                if a >= 4:
                    if a in (4, 5):
                        pe.wait_ge(columned, a - 3)
                    else:
                        pe.wait_ge(copied, a - 5)
                for b0, first, n in halves(a):
                    for b in range(n):
                        last = nc.tensor.transpose(b0[:, b * EP:(b + 1) * EP], array[:, (first + b) * P:(first + b + 1) * P],
                                                   k.ident[0:EP, 0:EP])
                last.then_inc(turned, 1)

        @block.scalar
        def _(act):
            act.wait_ge(edges_in, 128)
            nc.scalar.activation(sf[:, :], s_i[:, :], ACT.Copy).then_inc(floats_made, 1)
            act.wait_ge(ints_made, 1)
            nc.scalar.activation(high[:, :], high_i[:, :], ACT.Copy)
            nc.scalar.activation(low[:, :], low_i[:, :], ACT.Copy)
            act.wait_ge(ints_made, 2)
            nc.scalar.activation(lane[:, :], lane_i[:, :], ACT.Copy).then_inc(floats_made, 1)
            for a in range(2, len(ARRAYS)):
                act.wait_ge(turned, a + 1)
                for b0, first, n in halves(a):
                    last = nc.scalar.activation(by_raw(ARRAYS[a][1])[:, first:first + n, :],
                                                b0[:, 0:n * EP].rearrange("q (b p) -> q b p", p=EP), ACT.Copy)
                last.then_inc(copied, 1)

        @block.vector
        def _(dve):
            V = nc.vector
            n = [0]

            def step(ins):
                n[0] += 1
                ins.then_inc(made, 1)
                dve.wait_ge(made, n[0])
            V.memset(s_i[:, :], 0)
            V.memset(d_i[:, :], NO_EDGE).then_inc(padded, 1)
            V.memset(k.eps[:, :], EPS)
            V.memset(k.ones[:, :], 1.0)
            V.memset(k.tally[:, :], 0.0)
            V.memset(carry_row[:, :], 0.0)
            dve.wait_ge(consts, 7)
            dve.wait_ge(edges_in, 128)
            step(V.tensor_copy(df[:, :], d_i[:, :]))
            V.tensor_single_scalar(high_i[:, :], s_i[:, OWN], 8, op=ALU.logical_shift_right)
            V.tensor_single_scalar(low_i[:, :], s_i[:, OWN], 255, op=ALU.bitwise_and).then_inc(ints_made, 1)
            V.tensor_single_scalar(place_i[:, :], d_i[:, OWN], GROUP_NODES - 1, op=ALU.bitwise_and)
            step(V.tensor_single_scalar(group_i[:, :], d_i[:, HALO - 1:W], GROUP_NODES.bit_length() - 1, op=ALU.logical_shift_right))
            step(V.tensor_copy(group[:, :], group_i[:, :]))
            dve.wait_ge(floats_made, 1)
            V.tensor_tensor(step_up[:, :], df[:, 1:W + 1], df[:, 0:W], ALU.subtract)
            step(V.tensor_tensor(is_self[:, :], sf[:, :], df[:, 0:W], ALU.is_equal))
            step(V.scalar_tensor_tensor(drop[:, :], step_up[:, :], 0.0, is_self[:, :], ALU.not_equal, ALU.mult))
            step(V.tensor_tensor(drop_no[:, :], drop[:, :], number[:, :], ALU.mult))
            step(V.tensor_tensor_scan(last_drop[:, :], drop_no[:, :], drop_no[:, :], 0.0, ALU.max, ALU.max))
            step(V.tensor_tensor(m1[:, :], number[:, OWN], last_drop[:, BEFORE], ALU.subtract))
            step(V.tensor_tensor(degree[:, :], m1[:, :], drop[:, OWN], ALU.mult))
            V.tensor_reduce(extreme[:, 0:1], degree[:, :], AX.X, ALU.max)
            step(V.tensor_scalar(degree[:, :], degree[:, :], CAP, None, ALU.min))
            V.tensor_tensor(starts[:, :], group[:, 1:RUN + 1], group[:, 0:RUN], ALU.not_equal)
            step(V.scalar_tensor_tensor(kept_before[:, :], number[:, OWN], -1.0, df[:, OWN], ALU.add, ALU.subtract))
            step(V.tensor_tensor(starts[:, :], starts[:, :], kept_before[:, :], ALU.mult))
            V.tensor_tensor_scan(base[:, :], starts[:, :], starts[:, :], 0.0, ALU.max, ALU.max).then_inc(base_made, 1)
            dve.wait_ge(base_up, 1)
            step(V.tensor_copy(base_row[:, :], bank[0][0:1, 0:EP]))
            V.tensor_tensor_scan(carry_row[:, 1:EP + 1], base_row[:, :], base_row[:, :], 0.0, ALU.max, ALU.max).then_inc(carry_made, 1)
            step(V.scalar_tensor_tensor(keep[:, :], df[:, OWN], float(N_NODES), drop[:, OWN], ALU.is_lt, ALU.is_gt))
            V.tensor_reduce(extreme[:, 1:2], step_up[:, OWN], AX.X, ALU.min)
            V.tensor_tensor(m2[:, :], drop[:, OWN], df[:, OWN], ALU.mult)
            dve.wait_ge(carry_down, 1)
            step(V.tensor_copy(carry[:, :], bank[1][0:EP, 0:1]))
            step(V.scalar_tensor_tensor(behind[:, :], base[:, :], carry[:, :], kept_before[:, :], ALU.max, ALU.subtract))
            V.scalar_tensor_tensor(slot[:, :], group[:, 1:RUN + 1], float(GROUP_SLOTS), behind[:, :], ALU.mult, ALU.subtract)
            step(V.scalar_tensor_tensor(dev[:, :], behind[:, :], float(P), place_i[:, :], ALU.add, ALU.add))
            V.tensor_tensor(dev[:, :], dev[:, :], keep[:, :], ALU.mult)
            step(V.tensor_tensor(m1[:, :], slot[:, :], keep[:, :], ALU.mult))
            step(V.tensor_tensor(m1[:, :], m1[:, :], m2[:, :], ALU.add))
            step(V.tensor_scalar(target_i[:, :], m1[:, :], 0.0, float(NO_EDGE - 1), ALU.max, ALU.min))
            V.tensor_single_scalar(col_i[:, :], target_i[:, :], 7, op=ALU.logical_shift_right)
            step(V.tensor_single_scalar(lane_i[:, :], target_i[:, :], P - 1, op=ALU.bitwise_and))
            V.tensor_reduce(extreme[:, 2:3], dev[:, :], AX.X, ALU.max).then_inc(ints_made, 1)
            V.tensor_tensor(m1[:, :], dev[:, :], keep[:, :], ALU.subtract)
            V.scalar_tensor_tensor(col_s[:, :], keep[:, :], -FAR, col_i[:, :], ALU.mult, ALU.add)
            step(V.scalar_tensor_tensor(col_n[:, :], drop[:, OWN], -FAR, col_i[:, :], ALU.mult, ALU.add))
            V.tensor_reduce(extreme[:, 3:4], m1[:, :], AX.X, ALU.min)
            dve.wait_ge(floats_made, 2)
            V.tensor_scalar(dev[:, :], dev[:, :], CAP, -CAP, ALU.min, ALU.max).then_inc(arrays_made, 1)
            dve.wait_ge(arrays_made, 1)
            V.tensor_scalar(extreme[:, 0:1], extreme[:, 0:1], float(HALO), None, ALU.is_gt)
            V.tensor_scalar(extreme[:, 1:2], extreme[:, 1:2], 0.0, None, ALU.is_lt)
            V.tensor_scalar(extreme[:, 2:3], extreme[:, 2:3], 2.0 * P, None, ALU.is_gt)
            step(V.tensor_scalar(extreme[:, 3:4], extreme[:, 3:4], 0.0, None, ALU.is_lt))
            step(V.tensor_reduce(k.tally[0:EP, 0:1], extreme[:, :], AX.X, ALU.add))
            for a, (to, win) in enumerate(((k.rel_c[:, :, 0], win_s), (k.rel_c[:, :, 1], win_n))):
                step(V.tensor_scalar(win[:, :], win[:, :], -FAR, None, ALU.add))
                dve.wait_ge(turned, a + 1)
                for b0, first, m in halves(a):
                    last = V.tensor_tensor(by_raw(to)[:, first:first + m, :], b0[:, 0:m * EP].rearrange("q (b p) -> q b p", p=EP),
                                           by_raw(win)[:, first:first + m, :], ALU.subtract)
                last.then_inc(columned, 1)


def sort_edges(nc, x, table, keepers):
    k = keepers
    with ExitStack() as ctx:
        def sb(name, shape, dt=F32):
            return ctx.enter_context(nc.sbuf_tensor("b_" + name, shape, dt))

        def sem(name):
            return ctx.enter_context(nc.semaphore("b_" + name))

        grid = sb("grid", [P, 4, GRID])
        hot = sb("hot", [P, 2, RG, P], F16)
        hot_col = sb("hot_col", [P, 2, RG, 2, WIN], F16)
        spread = sb("spread", [P, 2, RG, 4, WIN], F16)
        nil = sb("nil", [P, P], F16)
        src_f, src_i, slane_i, stile_i = sb("src_f", [P, CHUNKS]), sb("src_i", [P, CHUNKS], I32), sb("slane_i", [P, CHUNKS], I32), sb("stile_i", [P, CHUNKS], I32)
        empty, filled, here = sb("empty", [P, CHUNKS]), sb("filled", [P, CHUNKS]), sb("here", [P, TILES])
        root, newton = sb("root", [P, TILES]), sb("newton", [P, TILES])
        y = sb("y", [P, 2, GN, D])
        whole_bank = [ctx.enter_context(nc.psum_tensor(f"b_bank{i}", [P, 512], F32)) for i in range(2)]
        bank = [b[:, 0:4 * SPAN].rearrange("p (a c) -> p a c", a=4) for b in whole_bank]
        padded, x_in, nil_made = sem("padded"), sem("x_in"), sem("nil_made")
        hots_made, columns_made, spread_made, placed, added, made = sem("hots_made"), sem("columns_made"), sem("spread_made"), sem("placed"), sem("added"), sem("made")
        deg_made, root_made, scaled = sem("deg_made"), sem("root_made"), sem("scaled")
        out_sem = [sem(f"table_out{j}") for j in range(2)]
        block = ctx.enter_context(nc.Block())
        XP = 65
        x_full = x[0:FULL_TILES * P, :].rearrange("(t p) d -> p t d", p=P)

        def rounds(eng, body):
            with eng.Fori(0, GROUPS // 2) as i:
                for j in range(2):
                    body(j, 2 * i + j)
            body(0, GROUPS - 1)

        @block.sync
        def _(sp):
            sp.wait_ge(padded, 1)
            for t in range(0, FULL_TILES, XP):
                sp.dma_start(k.xh[:, t:t + XP, :], x_full[:, t:t + XP, :]).then_inc(x_in, 16)
            sp.dma_start(k.xh[0:LAST_ROWS, FULL_TILES, :], x[FULL_TILES * P:N_NODES, :]).then_inc(x_in, 16)

            def store(j, g):
                sp.wait_ge(scaled, g + 1)
                sp.dma_start(table[:, bass.ds(g * (GN * D), GN * D)], y[:, j].rearrange("p t d -> p (t d)")).then_inc(out_sem[j], 16)
            rounds(sp, store)
            sp.wait_ge(out_sem[0], 16 * (GROUPS // 2 + 1))
            sp.wait_ge(out_sem[1], 16 * (GROUPS // 2))

        @block.gpsimd
        def _(pool):
            nc.gpsimd.memset(nil[:, :], 0.0).then_inc(nil_made, 1)

            def body(j, g):
                pool.wait_ge(placed, g + 1)
                pool.nop(nofuse=True)
                part = bass.ds(g * RG, RG)
                pool.wait_ge(columns_made, g + 1)
                pool.nop(nofuse=True)
                nc.gpsimd.tensor_tensor(spread[:, j, :, 0:3, :], hot_col[:, j, :, 0, :].unsqueeze(2).to_broadcast([P, RG, 3, WIN]),
                                        k.parts[:, part, :].unsqueeze(3).to_broadcast([P, RG, 3, WIN]), ALU.mult)
                nc.gpsimd.tensor_tensor(spread[:, j, :, 3, :], hot_col[:, j, :, 1, :], k.deg_r[:, part].unsqueeze(2).to_broadcast([P, RG, WIN]),
                                        ALU.mult).then_inc(spread_made, 1)
            rounds(pool, body)

        @block.tensor
        def _(pe):
            pe.wait_ge(nil_made, 1)
            nc.tensor.matmul(bank[0][:, :, :], nil[:, :], nil[:, 0:4 * SPAN].rearrange("p (a b) -> p a b", a=4), start=True, stop=True).then_inc(placed, 1)
            nc.tensor.matmul(bank[1][:, :, :], nil[:, :], nil[:, 0:4 * SPAN].rearrange("p (a b) -> p a b", a=4), start=True, stop=True).then_inc(placed, 1)

            def body(j, g):
                pe.wait_ge(added, g + 1)
                nc.tensor.matmul(bank[j][:, :, :], nil[:, :], nil[:, 0:4 * SPAN].rearrange("p (a b) -> p a b", a=4),
                                 start=True, stop=False, skip_group_check=True)
                pe.wait_ge(hots_made, g + 1)
                pe.wait_ge(spread_made, g + 1)
                for r in range(RG):
                    last = nc.tensor.matmul(bank[j][:, :, r // 2:r // 2 + WIN], hot[:, j, r], spread[:, j, r],
                                            start=False, stop=r == RG - 1, skip_group_check=True)
                last.then_inc(placed, 1)
            rounds(pe, body)

        @block.scalar
        def _(act):
            act.wait_ge(deg_made, 1)
            nc.scalar.activation(root[:, :], k.deg[:, :], ACT.Sqrt).then_inc(root_made, 1)

        @block.vector
        def _(dve):
            V = nc.vector
            V.memset(k.xh[:, FULL_TILES:TILES, :], 0.0).then_inc(padded, 1)
            V.memset(here[:, :], 0.0).then_inc(added, 1)
            V.memset(grid[:, :, :], 0.0).then_inc(added, 1)

            def add(j, g):
                dve.wait_ge(placed, g + 3)
                dve.wait_ge(added, g + 2)
                s, m = grid[:, 0:3, bass.ds(g * CG, SPAN)], grid[:, 3, bass.ds(g * GN, SPAN)]
                V.tensor_tensor(s, s, bank[j][:, 0:3, :], ALU.add)
                V.tensor_tensor(m, m, bank[j][:, 3, :], ALU.add).then_inc(added, 1)

            def hots(j, g):
                dve.wait_ge(placed, g + 1)
                columns(j, g)
                for r in range(RG):
                    last = V.tensor_scalar(hot[:, j, r], k.place16[:, 0:P], k.lane_r[:, bass.ds(g * RG + r, 1)], None, ALU.is_equal)
                last.then_inc(hots_made, 1)

            def columns(j, g):
                V.tensor_tensor(hot_col[:, j], k.place16[:, 0:WIN].unsqueeze(1).unsqueeze(1).to_broadcast([P, RG, 2, WIN]),
                                k.rel_c[:, bass.ds(g * RG, RG), :].unsqueeze(3).to_broadcast([P, RG, 2, WIN]), ALU.is_equal).then_inc(columns_made, 1)
            hots(0, 0)
            with dve.Fori(0, GROUPS // 2) as i:
                for j in range(2):
                    hots(1 - j, 2 * i + (j + 1))
                    add(j, 2 * i + j)
            add(0, GROUPS - 1)
            n = [0]

            def step(ins):
                n[0] += 1
                ins.then_inc(made, 1)
                dve.wait_ge(made, n[0])
            dve.wait_ge(added, GROUPS + 2)
            slots, nodes = slice(BACK, BACK + CHUNKS), slice(BACK, BACK + TILES)
            V.tensor_scalar(here[:, :], grid[:, 3, nodes], 1.0, None, ALU.is_ge)
            V.tensor_scalar(k.deg[:, :], grid[:, 3, nodes], 1.0, None, ALU.max).then_inc(deg_made, 1)
            step(V.scalar_tensor_tensor(src_f[:, :], grid[:, 0, slots], 256.0, grid[:, 1, slots], ALU.mult, ALU.add))
            step(V.tensor_scalar(src_i[:, :], src_f[:, :], 0.0, float(N_NODES - 1), ALU.max, ALU.min))
            V.tensor_single_scalar(slane_i[:, :], src_i[:, :], P - 1, op=ALU.bitwise_and)
            V.tensor_single_scalar(stile_i[:, :], src_i[:, :], 7, op=ALU.logical_shift_right)
            V.tensor_scalar(empty[:, :], grid[:, 2, slots], 0.0, FAR, ALU.is_equal, ALU.mult)
            step(V.tensor_scalar(filled[:, :], grid[:, 2, slots], 1.0, None, ALU.is_ge))
            V.scalar_tensor_tensor(k.row_i[:, :], slane_i[:, :], float(TILES), stile_i[:, :], ALU.mult, ALU.add)
            V.scalar_tensor_tensor(k.rel[:, :], grid[:, 2, slots], k.lane_no[:, :], empty[:, :], ALU.add, ALU.add)
            V.tensor_tensor(k.src_lane[:, :], slane_i[:, :], empty[:, :], ALU.add)
            V.tensor_copy(k.src_tile[:, :], stile_i[:, :])
            V.tensor_reduce(k.tally[:, 1:2], filled[:, :], AX.X, ALU.add)
            V.tensor_reduce(k.tally[:, 2:3], here[:, :], AX.X, ALU.add)
            dve.wait_ge(root_made, 1)
            step(V.reciprocal(k.norm[:, :], root[:, :]))
            step(V.tensor_tensor(newton[:, :], k.norm[:, :], k.norm[:, :], ALU.mult))
            step(V.tensor_tensor(newton[:, :], newton[:, :], k.deg[:, :], ALU.mult))
            step(V.tensor_scalar(newton[:, :], newton[:, :], -0.5, 1.5, ALU.mult, ALU.add))
            step(V.tensor_tensor(k.norm[:, :], k.norm[:, :], newton[:, :], ALU.mult))
            V.tensor_tensor(k.norm2[:, :], k.norm[:, :], k.norm[:, :], ALU.mult)
            dve.wait_ge(x_in, 16 * (FULL_TILES // XP + 1))

            def scale(j, g, stores):
                if stores is not None:
                    dve.wait_ge(out_sem[j], stores)
                V.tensor_tensor(y[:, j], k.xh[:, bass.ds(g * GN, GN), :],
                                k.norm[:, bass.ds(g * GN, GN)].unsqueeze(2).to_broadcast([P, GN, D]), ALU.mult).then_inc(scaled, 1)
            for j in range(2):
                scale(j, j, None)
            with dve.Fori(1, GROUPS // 2) as i:
                for j in range(2):
                    scale(j, 2 * i + j, 16 * i)
            scale(0, GROUPS - 1, 16 * (GROUPS // 2))


def layers(nc, x, out, tables, flag, keepers):
    k = keepers
    with ExitStack() as ctx:
        def sb(name, shape, dt=F32):
            return ctx.enter_context(nc.sbuf_tensor("c_" + name, shape, dt))

        def sem(name):
            return ctx.enter_context(nc.semaphore("c_" + name))

        row_s = sb("row_s", [P, 2, CG], I32)
        rows = sb("rows", [P, 2, CG, D])
        sel = sb("sel", [P, 2, sum(WIDTH)])
        uv = sb("uv", [P, 2, GN, 2, D])
        sums, own, x_c = sb("sums", [P, GN, D]), sb("own", [P, GN, D]), sb("x_c", [P, GN, D])
        uvt = sb("uvt", [P, GN, P])
        y = sb("y", [P, 2, GN, D])
        res = sb("res", [P, 2, GN, D])
        z, sq = sb("z", [P, GN, D]), sb("sq", [P, GN, D])
        mean, var, std, rstd = (sb(n, [P, GN]) for n in ("mean", "var", "std", "rstd"))
        hot_l, hot_t = sb("hot_l", [P, CG, P], F16), sb("hot_t", [P, CG, TILES], F16)
        nil = sb("nil", [P, TILES], F16)
        count = sb("count", [P, TILES])
        totals, bad = sb("totals", [1, 4]), sb("bad", [1, 4])
        p_sum = [ctx.enter_context(nc.psum_tensor(f"c_sum{i}", [P, GN, D], F32)) for i in range(2)]
        p_turn = [ctx.enter_context(nc.psum_tensor(f"c_turn{i}", [P, 4, P], F32)) for i in range(2)]
        p_out = [ctx.enter_context(nc.psum_tensor(f"c_out{i}", [P, GN, D], F32)) for i in range(2)]
        p_count = ctx.enter_context(nc.psum_tensor("c_p_count", [P, 512], F32))
        p_tally = ctx.enter_context(nc.psum_tensor("c_p_tally", [1, 512], F32))
        staged, issued = sem("staged"), sem("issued")
        BATCH = 3
        NB = CG // BATCH
        gathered = [[sem(f"gathered{j}{b}") for b in range(NB)] for j in range(2)]
        sel_made, summed, own_made, uv_made, turned, uvt_made, multiplied = (
            sem(n) for n in ("sel_made", "summed", "own_made", "uv_made", "turned", "uvt_made", "multiplied"))
        z_made, centred, squared, var_made, std_made, y_made, made = (sem(n) for n in ("z_made", "centred", "squared", "var_made", "std_made", "y_made", "made"))
        hots_made, counted, nil_made, tally_made, tallied = sem("hots_made"), sem("counted"), sem("nil_made"), sem("tally_made"), sem("tallied")
        stored = [sem(f"stored{j}") for j in range(2)]
        res_in = [sem(f"res_in{j}") for j in range(2)]
        block = ctx.enter_context(nc.Block())
        x_full = x[0:FULL_TILES * P, :].rearrange("(t p) d -> p t d", p=P)
        out_full = out[0:FULL_TILES * P, :].rearrange("(t p) d -> p t d", p=P)
        per_layer = lambda j: GROUPS // 2 + 1 - j

        def at_least(eng, s, v):
            if not (isinstance(v, int) and v <= 0):
                eng.wait_ge(s, v)

        def steps(eng, body, last=GROUPS + 2):
            for t in range(4):
                body(t, t % 2)
            with eng.Fori(2, GROUPS // 2) as i:
                for j in range(2):
                    body(2 * i + j, j)
            for t in range(GROUPS - 1, last):
                body(t, t % 2)

        def live(t, back):
            return not isinstance(t, int) or 0 <= t - back < GROUPS

        def group(g):
            return bass.ds(g * GN, GN)

        def before(t, l):
            return GROUPS if l == 1 and isinstance(t, int) and t < 2 else t + (GROUPS * l - 1)

        @block.sync
        def _(sp):
            for l in range(2):
                def body(t, j, l=l):
                    g = t - 2
                    if l == 1 and live(t, 2):
                        sp.wait_ge(y_made, GROUPS + 1 + g)
                        if isinstance(g, int) and g == GROUPS - 1:
                            n = FULL_TILES - g * GN
                            sp.dma_start(out_full[:, g * GN:FULL_TILES, :], y[:, j, 0:n]).then_inc(stored[j], 16)
                            sp.dma_start(out[FULL_TILES * P:N_NODES, :], y[0:LAST_ROWS, j, n]).then_inc(stored[j], 16)
                        else:
                            sp.dma_start(out_full[:, group(g), :], y[:, j]).then_inc(stored[j], 16)
                    if l == 0 and live(t, 2):
                        sp.wait_ge(y_made, g + 1)
                        sp.dma_start(tables[1][:, bass.ds(g * (GN * D), GN * D)], y[:, j].rearrange("p t d -> p (t d)")).then_inc(stored[j], 16)
                    if l == 1 and live(t, 0):
                        at_least(sp, z_made, t - 1)
                        if not isinstance(t, int):
                            sp.nop(nofuse=True)
                        if isinstance(t, int) and t == GROUPS - 1:
                            n = FULL_TILES - t * GN
                            sp.dma_start(res[:, j, 0:n], x_full[:, t * GN:FULL_TILES, :]).then_inc(res_in[j], 16)
                            sp.dma_start(res[0:LAST_ROWS, j, n], x[FULL_TILES * P:N_NODES, :]).then_inc(res_in[j], 16)
                        else:
                            sp.dma_start(res[:, j], x_full[:, group(t), :]).then_inc(res_in[j], 16)
                steps(sp, body)
            for j in range(2):
                sp.wait_ge(stored[j], 16 * (2 * per_layer(j) + (1 - j)))

        @block.gpsimd
        def _(pool):
            nc.gpsimd.memset(nil[:, :], 0.0).then_inc(nil_made, 1)
            for l in range(2):
                table = tables[l].rearrange("p (t d) -> (p t) d", d=D)
                if l == 1:
                    for j in range(2):
                        pool.wait_ge(stored[j], 16 * per_layer(j))
                def body(t, j, l=l, table=table):
                    if not live(t, 0):
                        return
                    pool.wait_ge(staged, GROUPS * l + 1 + t)
                    pool.nop(nofuse=True)
                    at_least(pool, summed, before(t, l))
                    pool.nop(nofuse=True)
                    for c in range(CG):
                        pool.indirect_dma_start(out=rows[:, j, c], out_offset=None, in_=table,
                                                in_offset=bass.IndirectOffsetOnAxis(ap=row_s[:, j, c:c + 1], axis=0)
                                                ).then_inc(gathered[j][c // BATCH], 16)
                steps(pool, body, last=GROUPS)

        @block.tensor
        def _(pe):
            pe.wait_ge(nil_made, 1)
            nc.tensor.matmul(p_count[:, 0:TILES], nil[:, 0:P], nil[:, :], start=True, stop=False, skip_group_check=True)
            for l in range(2):
                def body(t, j, l=l):
                    if live(t, 0):
                        at_least(pe, uv_made, before(t, l))
                        for b in range(NB):
                            pe.wait_ge(sel_made, NB * t + (NB * GROUPS * l + b + 1))
                            if isinstance(t, int):
                                pe.wait_ge(gathered[j][b], 16 * BATCH * (per_layer(j) * l + t // 2 + 1))
                            else:
                                pe.wait_ge(gathered[j][b], (t - j) * (8 * BATCH) + 16 * BATCH * (per_layer(j) * l + 1))
                            for c in range(BATCH * b, BATCH * (b + 1)):
                                for n, tile in enumerate(REACH[c]):
                                    last = nc.tensor.matmul(p_sum[j][:, tile, :], sel[:, j, START[c] + n * P:START[c] + (n + 1) * P],
                                                            rows[:, j, c], start=c == 0 and n == 0, stop=c == CG - 1, skip_group_check=True)
                        last.then_inc(summed, 1)
                    if live(t, 2):
                        pe.wait_ge(uvt_made, GROUPS * l - 1 + t)
                        at_least(pe, z_made if l else y_made, t - 3)
                        for tile in range(GN):
                            last = nc.tensor.matmul(p_out[j][:, tile, :], uvt[:, tile, :], k.wcat[:, l, :], start=True, stop=True)
                        last.then_inc(multiplied, 1)
                    if live(t, 1):
                        pe.wait_ge(uv_made, GROUPS * l + t)
                        for tile in range(GN):
                            last = nc.tensor.transpose(p_turn[tile // 4][:, tile % 4, :],
                                                       uv[:, 1 - j, tile].rearrange("p a d -> p (a d)"), k.ident[:, :])
                        last.then_inc(turned, 1)
                    if l == 0 and live(t, 0):
                        pe.wait_ge(hots_made, t + 1)
                        for c in range(CG):
                            last = nc.tensor.matmul(p_count[:, 0:TILES], hot_l[:, c], hot_t[:, c], start=False, stop=False, skip_group_check=True)
                        last.then_inc(counted, 1)
                steps(pe, body)
            nc.tensor.matmul(p_count[:, 0:TILES], nil[:, 0:P], nil[:, :], start=False, stop=True, skip_group_check=True).then_inc(counted, 1)
            pe.wait_ge(tally_made, 1)
            nc.tensor.matmul(p_tally[0:1, 0:4], k.ones[:, :], k.tally[:, :], start=True, stop=True).then_inc(tallied, 1)

        @block.scalar
        def _(act):
            for l in range(2):
                def body(t, j, l=l):
                    if live(t, 1):
                        act.wait_ge(turned, GROUPS * l + t)
                        for h in range(2):
                            last = nc.scalar.activation(uvt[:, 4 * h:4 * h + 4, :], p_turn[h][:, :, :], ACT.Copy)
                        last.then_inc(uvt_made, 1)
                    if l == 1 and live(t, 2):
                        act.wait_ge(centred, t - 1)
                        nc.scalar.activation(sq[:, :, :], z[:, :, :], ACT.Square).then_inc(squared, 1)
                        act.wait_ge(var_made, t - 1)
                        nc.scalar.activation(std[:, :], var[:, :], ACT.Sqrt, bias=k.eps[:, :], scale=1.0 / D).then_inc(std_made, 1)
                steps(act, body)

        @block.vector
        def _(dve):
            V = nc.vector
            V.memset(res[:, :, :, :], 0.0)
            over = lambda a, g: a[:, group(g)].unsqueeze(2).to_broadcast([P, GN, D])
            along = lambda a: a[:, :].unsqueeze(2).to_broadcast([P, GN, D])
            done = [0]

            for l in range(2):
                def select(t, j, l=l):
                    at_least(dve, summed, before(t, l))
                    dve.nop(nofuse=True)
                    V.tensor_copy(row_s[:, j, :], k.row_i[:, bass.ds(t * CG, CG)]).then_inc(staged, 1)
                    for c in range(CG):
                        last = V.tensor_scalar(sel[:, j, START[c]:START[c] + WIDTH[c]], k.place[:, SKIP[c]:SKIP[c] + WIDTH[c]],
                                               k.rel[:, bass.ds(t * CG + c, 1)], None, ALU.is_equal)
                        if c % BATCH == BATCH - 1:
                            last.then_inc(sel_made, 1)

                select(0, 0)
                def body(t, j, l=l):
                    m = [0]

                    def step(ins):
                        m[0] += 1
                        ins.then_inc(made, 1)
                        dve.wait_ge(made, t * K + (done[0] + m[0]))

                    def skip(n):
                        for _ in range(n):
                            m[0] += 1
                            dve.sem_inc(made, 1)
                    if live(t, 1):
                        g = t - 1
                        h = k.xh[:, group(g), :]
                        step(V.tensor_tensor(own[:, :, :], h, over(k.norm2, g), ALU.mult))
                        dve.wait_ge(summed, GROUPS * l + t)
                        step(V.tensor_tensor(sums[:, :, :], p_sum[1 - j][:, :, :], over(k.norm, g), ALU.mult))
                        step(V.tensor_tensor(sums[:, :, :], sums[:, :, :], own[:, :, :], ALU.add))
                        at_least(dve, turned, GROUPS * l + t - 2)
                        V.tensor_tensor(uv[:, 1 - j, :, 0, :], sums[:, :, :], h, ALU.add)
                        V.tensor_tensor(uv[:, 1 - j, :, 1, :], sums[:, :, :], h, ALU.mult).then_inc(uv_made, 1)
                        dve.wait_ge(uv_made, GROUPS * l + t)
                    else:
                        skip(3)
                    if live(t, -1):
                        select(t + 1, 1 - j)
                    if live(t, 2):
                        g = t - 2
                        dve.wait_ge(multiplied, GROUPS * l - 1 + t)
                        if l == 0:
                            h = k.xh[:, group(g), :]
                            step(V.tensor_scalar(h, p_out[j][:, :, :], 0.0, None, ALU.max))
                            if isinstance(t, int):
                                at_least(dve, stored[j], 16 * (g // 2))
                            else:
                                dve.wait_ge(stored[j], (t - j) * 8 - 16)
                            V.tensor_tensor(y[:, j], h, over(k.norm, g), ALU.mult).then_inc(y_made, 1)
                        else:
                            if isinstance(t, int):
                                dve.wait_ge(res_in[j], 16 * (g // 2 + 1 + (1 if g == GROUPS - 1 else 0)))
                            else:
                                dve.wait_ge(res_in[j], (t - j) * 8)
                            dve.wait_ge(y_made, GROUPS - 2 + t)
                            V.tensor_tensor(z[:, :, :], res[:, j], p_out[j][:, :, :], ALU.add).then_inc(z_made, 1)
                            dve.wait_ge(z_made, t - 1)
                            step(V.tensor_reduce(mean[:, :], z[:, :, :], AX.X, ALU.add))
                            step(V.tensor_scalar(mean[:, :], mean[:, :], 1.0 / D, None, ALU.mult))
                            V.tensor_tensor(z[:, :, :], z[:, :, :], along(mean), ALU.subtract).then_inc(centred, 1)
                            dve.wait_ge(squared, t - 1)
                            V.tensor_reduce(var[:, :], sq[:, :, :], AX.X, ALU.add).then_inc(var_made, 1)
                            dve.wait_ge(std_made, t - 1)
                            step(V.reciprocal(rstd[:, :], std[:, :]))
                            if isinstance(t, int):
                                at_least(dve, stored[j], 16 * (g // 2) + 16 * per_layer(j))
                            else:
                                dve.wait_ge(stored[j], (t - j) * 8 - 16 + 16 * per_layer(j))
                            V.tensor_tensor(y[:, j], z[:, :, :], along(rstd), ALU.mult).then_inc(y_made, 1)
                    if l == 0 and live(t, 0):
                        at_least(dve, counted, t)
                        for c in range(CG):
                            V.tensor_scalar(hot_l[:, c], k.place16[:, 0:P], k.src_lane[:, bass.ds(t * CG + c, 1)], None, ALU.is_equal)
                            last = V.tensor_scalar(hot_t[:, c], k.place16[:, :], k.src_tile[:, bass.ds(t * CG + c, 1)], None, ALU.is_equal)
                        last.then_inc(hots_made, 1)
                K = 4 if l == 0 else 6

                def whole(t, j, body=body, l=l):
                    body(t, j)
                    if isinstance(t, int) and not live(t, 2):
                        dve.sem_inc(made, K - 3)
                steps(dve, whole)
                done[0] += K * (GROUPS + 2)
            dve.wait_ge(counted, GROUPS + 1)
            n = [done[0]]

            def step(ins):
                n[0] += 1
                ins.then_inc(made, 1)
                dve.wait_ge(made, n[0])
            step(V.scalar_tensor_tensor(count[:, :], p_count[:, 0:TILES], 1.0, k.deg[:, :], ALU.add, ALU.not_equal))
            V.tensor_reduce(k.tally[:, 3:4], count[:, :], AX.X, ALU.add).then_inc(tally_made, 1)
            dve.wait_ge(tallied, 1)
            step(V.tensor_copy(totals[:, :], p_tally[0:1, 0:4]))
            for c, want in enumerate((0, N_EDGES - N_NODES, N_NODES, 0)):
                last = V.tensor_scalar(bad[:, c:c + 1], totals[:, c:c + 1], float(want), None, ALU.not_equal)
            step(last)
            step(V.tensor_reduce(flag[:, :], bad[:, :], AX.X, ALU.add))


GP = 125
G_CHUNKS = N_EDGES // GP
G_TILES = N_NODES // GP
G_GROUP = 8
G_GROUPS = G_TILES // G_GROUP
assert G_CHUNKS * GP == N_EDGES and G_GROUPS * G_GROUP * GP == N_NODES
G_DRAM = {"g_table": (N_NODES, D), "g_hidden": (N_NODES, D), "g_sums": (N_NODES + GP, D),
          "g_deg0": (N_NODES + GP, 1), "g_deg1": (N_NODES + GP, 1)}


def general_path(nc, x, src, dst, weights, out, dram, run_if):
    with ExitStack() as ctx:
        def sb(name, shape, dt=F32):
            return ctx.enter_context(nc.sbuf_tensor("g_" + name, shape, dt))

        def sem(name):
            return ctx.enter_context(nc.semaphore("g_" + name))

        ident, before = sb("ident", [GP, GP]), sb("before", [GP, GP])
        spare_i, spare = sb("spare_i", [GP, 1], I32), sb("spare", [GP, 1])
        ones, zero, eps = sb("ones", [GP, 1]), sb("zero", [GP, G_GROUP * D]), sb("eps", [GP, 1])
        wcat = sb("wcat", [2 * D, 2, D])
        key_i, key, key_b = sb("key_i", [GP, 1], I32), sb("key", [GP, 1]), sb("key_b", [GP, GP])
        from_i = sb("from_i", [GP, 1], I32)
        same, same_before = sb("same", [GP, GP]), sb("same_before", [GP, GP])
        n_before, first, shifted, to_f = (sb(n, [GP, 1]) for n in ("n_before", "first", "shifted", "to_f"))
        to_i = sb("to_i", [GP, 1], I32)
        rows, total = sb("rows", [GP, D]), sb("total", [GP, D])
        deg, root, norm, newton = (sb(n, [GP, 2, G_TILES]) for n in ("deg", "root", "norm", "newton"))
        xg, sg, yg, zg, sq = (sb(n, [GP, G_GROUP, D]) for n in ("xg", "sg", "yg", "zg", "sq"))
        uv, uvt = sb("uv", [GP, G_GROUP, 2, D]), sb("uvt", [P, G_GROUP, GP])
        mean, var, std, rstd = (sb(n, [GP, G_GROUP]) for n in ("mean", "var", "std", "rstd"))
        res = sb("res", [GP, G_GROUP, D])
        p_row = ctx.enter_context(nc.psum_tensor("g_p_row", [GP, 512], F32))
        p_sum = ctx.enter_context(nc.psum_tensor("g_p_sum", [GP, 512], F32))
        p_turn = [ctx.enter_context(nc.psum_tensor(f"g_p_turn{h}", [P, 512], F32)) for h in range(2)]
        p_out = ctx.enter_context(nc.psum_tensor("g_p_out", [GP, 512], F32))

        made, consts, cleared, w_in = sem("made"), sem("consts"), sem("cleared"), sem("w_in")
        key_in, key_spread, key_turned, same_made = sem("key_in"), sem("key_spread"), sem("key_turned"), sem("same_made")
        gathered, summed, total_made, added = sem("gathered"), sem("summed"), sem("total_made"), sem("added")
        deg_in, deg_made, rooted = sem("deg_in"), sem("deg_made"), sem("rooted")
        group_in, sums_in, uv_made, turned, uvt_made = sem("group_in"), sem("sums_in"), sem("uv_made"), sem("turned"), sem("uvt_made")
        multiplied, act_made, centred, squared = sem("multiplied"), sem("act_made"), sem("centred"), sem("squared")
        var_made, std_made, group_made, group_out = sem("var_made"), sem("std_made"), sem("group_made"), sem("group_out")
        hidden_out = sem("hidden_out")
        block = ctx.enter_context(nc.Block())

        by_lane = "(p t) d -> p t d"
        xv, ov = x.rearrange(by_lane, p=GP), out.rearrange(by_lane, p=GP)
        tv, hv = dram["g_table"].rearrange(by_lane, p=GP), dram["g_hidden"].rearrange(by_lane, p=GP)
        sv = dram["g_sums"][0:N_NODES, :].rearrange(by_lane, p=GP)
        PASSES = [(src, dram["g_deg0"], False), (dst, dram["g_deg1"], False),
                  (dst, dram["g_sums"], True), (dst, dram["g_sums"], True)]

        @block.sync
        def _(sp):
            with run_if(sp):
                for l in range(2):
                    for k in range(2):
                        sp.dma_start(wcat[k * D:(k + 1) * D, l, :], weights[2 * l + k]).then_inc(w_in, 16)

                def keys(n):
                    with sp.Fori(0, G_CHUNKS) as c:
                        sp.dma_start(key_i[:, :], PASSES[n][0][bass.ds(c * GP, GP)].unsqueeze(1)).then_inc(key_in, 16)
                        sp.dma_start(from_i[:, :], src[bass.ds(c * GP, GP)].unsqueeze(1)).then_inc(key_in, 16)
                        sp.wait_ge(added, 16 * c + 16 * (1 + n * G_CHUNKS))
                        sp.nop(nofuse=True)

                part = lambda g: bass.ds(g * G_GROUP, G_GROUP)
                keys(0)
                keys(1)
                sp.wait_ge(added, 16 * 2 * G_CHUNKS)
                for k in range(2):
                    sp.dma_start(deg[:, k, :], dram[f"g_deg{k}"][0:N_NODES, :].rearrange("(p t) one -> p (t one)", p=GP)).then_inc(deg_in, 16)
                with sp.Fori(0, G_GROUPS) as g:
                    sp.dma_start(xg[:, :, :], xv[:, part(g), :]).then_inc(group_in, 16)
                    sp.wait_ge(group_made, g + 1)
                    sp.dma_start(tv[:, part(g), :], yg[:, :, :]).then_inc(group_out, 16)
                    sp.wait_ge(group_out, 16 * g + 16)
                    sp.nop(nofuse=True)
                for l in range(2):
                    keys(2 + l)
                    sp.wait_ge(added, 16 * (3 + l) * G_CHUNKS)
                    done = G_GROUPS * (1 + l)
                    with sp.Fori(0, G_GROUPS) as g:
                        sp.dma_start(xg[:, :, :], (xv if l == 0 else hv)[:, part(g), :]).then_inc(group_in, 16)
                        sp.dma_start(res[:, :, :], xv[:, part(g), :]).then_inc(group_in, 16)
                        sp.dma_start(sg[:, :, :], sv[:, part(g), :]).then_inc(group_in, 16)
                        sp.wait_ge(group_made, g + (1 + done))
                        sp.dma_start((tv if l == 0 else ov)[:, part(g), :], yg[:, :, :]).then_inc(group_out, 16)
                        if l == 0:
                            sp.dma_start(hv[:, part(g), :], zg[:, :, :]).then_inc(hidden_out, 16)
                            sp.wait_ge(hidden_out, 16 * g + 16)
                            sp.nop(nofuse=True)
                        sp.wait_ge(group_out, 16 * g + 16 * (1 + done))
                        sp.nop(nofuse=True)

        @block.gpsimd
        def _(pool):
            with run_if(pool):
                nc.gpsimd.memset(ident[:, :], 0.0).then_inc(consts, 1)
                nc.gpsimd.memset(before[:, :], 1.0).then_inc(consts, 1)
                nc.gpsimd.memset(zero[:, :], 0.0).then_inc(consts, 1)
                nc.gpsimd.iota(spare_i[:, :], pattern=[[1, 1]], base=N_NODES, channel_multiplier=1).then_inc(consts, 1)
                pool.wait_ge(consts, 4)
                nc.gpsimd.affine_select(out=ident[:, :], in_=ident[:, :], compare_op=ALU.not_equal, fill=1.0,
                                        base=0, pattern=[[-1, GP]], channel_multiplier=1).then_inc(consts, 1)
                nc.gpsimd.affine_select(out=before[:, :], in_=before[:, :], compare_op=ALU.is_gt, fill=0.0,
                                        base=0, pattern=[[-1, GP]], channel_multiplier=1).then_inc(consts, 1)

                def clear_sums():
                    with pool.Fori(0, G_GROUPS) as g:
                        pool.dma_start(sv[:, bass.ds(g * G_GROUP, G_GROUP), :],
                                       zero[:, :].rearrange("p (t d) -> p t d", d=D)).then_inc(cleared, 16)
                for k in range(2):
                    pool.dma_start(dram[f"g_deg{k}"][0:N_NODES, :].rearrange("(p t) one -> p (t one)", p=GP),
                                   zero[:, 0:G_TILES]).then_inc(cleared, 16)
                    pool.dma_start(dram[f"g_deg{k}"][N_NODES:, :], zero[:, 0:1]).then_inc(cleared, 16)
                clear_sums()
                pool.dma_start(dram["g_sums"][N_NODES:, :], zero[:, 0:D]).then_inc(cleared, 16)
                pool.wait_ge(cleared, 16 * (5 + G_GROUPS))
                for n, (_, into, gather) in enumerate(PASSES):
                    done = n * G_CHUNKS
                    if n == 3:
                        pool.wait_ge(group_in, 16 * 4 * G_GROUPS)
                        clear_sums()
                        pool.wait_ge(cleared, 16 * (5 + 2 * G_GROUPS))
                    with pool.Fori(0, G_CHUNKS) as c:
                        if gather:
                            pool.wait_ge(key_in, 32 * c + 32 * (1 + done))
                            pool.nop(nofuse=True)
                            pool.wait_ge(group_out, 16 * G_GROUPS * (n - 1))
                            pool.indirect_dma_start(out=rows[:, :], out_offset=None, in_=dram["g_table"],
                                                    in_offset=bass.IndirectOffsetOnAxis(ap=from_i[:, :], axis=0)).then_inc(gathered, 16)
                        pool.wait_ge(total_made, c + (1 + done))
                        pool.nop(nofuse=True)
                        pool.indirect_dma_start(out=into, out_offset=bass.IndirectOffsetOnAxis(ap=to_i[:, :], axis=0),
                                                in_=total[:, 0:D if gather else 1], in_offset=None, compute_op=ALU.add).then_inc(added, 16)
                        pool.wait_ge(added, 16 * c + 16 * (1 + done))
                        pool.nop(nofuse=True)

        @block.tensor
        def _(pe):
            with run_if(pe):
                pe.wait_ge(consts, 6)
                pe.wait_ge(w_in, 64)

                def edges(n):
                    done, gather = n * G_CHUNKS, PASSES[n][2]
                    with pe.Fori(0, G_CHUNKS) as c:
                        pe.wait_ge(key_spread, c + (1 + done))
                        nc.tensor.matmul(p_row[:, 0:GP], key_b[:, :], ident[:, :], start=True, stop=True).then_inc(key_turned, 1)
                        pe.wait_ge(same_made, c + (1 + done))
                        if gather:
                            pe.wait_ge(gathered, 16 * c + 16 * (1 + (n - 2) * G_CHUNKS))
                            nc.tensor.matmul(p_sum[:, 0:D], same[:, :], rows[:, :], start=True, stop=True).then_inc(summed, 1)
                        else:
                            nc.tensor.matmul(p_sum[:, 0:1], same[:, :], ones[:, :], start=True, stop=True).then_inc(summed, 1)
                edges(0)
                edges(1)
                for l in range(2):
                    edges(2 + l)
                    with pe.Fori(0, G_GROUPS) as g:
                        pe.wait_ge(uv_made, g + (1 + l * G_GROUPS))
                        for t in range(G_GROUP):
                            last = nc.tensor.transpose(p_turn[t // 4][:, (t % 4) * GP:(t % 4 + 1) * GP],
                                                       uv[:, t].rearrange("p a d -> p (a d)"), ident[:, :])
                        last.then_inc(turned, 1)
                        pe.wait_ge(uvt_made, g + (1 + l * G_GROUPS))
                        for t in range(G_GROUP):
                            last = nc.tensor.matmul(p_out[:, t * D:(t + 1) * D], uvt[:, t, :], wcat[:, l, :], start=True, stop=True)
                        last.then_inc(multiplied, 1)

        @block.scalar
        def _(act):
            with run_if(act):
                act.wait_ge(deg_made, 1)
                nc.scalar.activation(root[:, :, :], deg[:, :, :], ACT.Sqrt).then_inc(rooted, 1)
                for l in range(2):
                    with act.Fori(0, G_GROUPS) as g:
                        act.wait_ge(turned, g + (1 + l * G_GROUPS))
                        nc.scalar.activation(uvt[:, 0:4, :], p_turn[0][:, 0:4 * GP].rearrange("p (t n) -> p t n", n=GP), ACT.Copy)
                        nc.scalar.activation(uvt[:, 4:8, :], p_turn[1][:, 0:4 * GP].rearrange("p (t n) -> p t n", n=GP),
                                             ACT.Copy).then_inc(uvt_made, 1)
                        if l == 1:
                            act.wait_ge(centred, g + 1)
                            nc.scalar.activation(sq[:, :, :], zg[:, :, :], ACT.Square).then_inc(squared, 1)
                            act.wait_ge(var_made, g + 1)
                            nc.scalar.activation(std[:, :], var[:, :], ACT.Sqrt, bias=eps[:, :], scale=1.0 / D).then_inc(std_made, 1)

        @block.vector
        def _(dve):
            with run_if(dve):
                V = nc.vector
                V.memset(ones[:, :], 1.0)
                V.memset(eps[:, :], EPS)
                dve.wait_ge(consts, 6)
                V.tensor_copy(spare[:, :], spare_i[:, :]).then_inc(made, 1)
                dve.wait_ge(made, 1)
                count = [1]

                def stepper(base, per_round, i):
                    n = [0]

                    def step(ins):
                        n[0] += 1
                        ins.then_inc(made, 1)
                        dve.wait_ge(made, i * per_round + (base + n[0]))
                    return step, n

                def edges(n):
                    done, gather = n * G_CHUNKS, PASSES[n][2]
                    K = 8
                    with dve.Fori(0, G_CHUNKS) as c:
                        step, k = stepper(count[0], K, c)
                        dve.wait_ge(key_in, 32 * c + 32 * (1 + done))
                        step(V.tensor_copy(key[:, :], key_i[:, :]))
                        V.tensor_copy(key_b[:, :], key[:, :].to_broadcast([GP, GP])).then_inc(key_spread, 1)
                        step(V.tensor_tensor(shifted[:, :], key[:, :], spare[:, :], ALU.subtract))
                        dve.wait_ge(key_turned, c + (1 + done))
                        step(V.tensor_scalar(same[:, :], p_row[:, 0:GP], key[:, :], None, ALU.is_equal))
                        V.tensor_copy(total[:, 0:1], ones[:, :]).then_inc(same_made, 1)
                        step(V.tensor_tensor(same_before[:, :], same[:, :], before[:, :], ALU.mult))
                        step(V.tensor_reduce(n_before[:, :], same_before[:, :], AX.X, ALU.add))
                        step(V.tensor_scalar(first[:, :], n_before[:, :], 0.0, None, ALU.is_equal))
                        step(V.scalar_tensor_tensor(to_f[:, :], shifted[:, :], first[:, :], spare[:, :], ALU.mult, ALU.add))
                        step(V.tensor_copy(to_i[:, :], to_f[:, :]))
                        dve.wait_ge(summed, c + (1 + done))
                        w = D if gather else 1
                        V.tensor_copy(total[:, 0:w], p_sum[:, 0:w]).then_inc(total_made, 1)
                        assert k[0] == K
                    count[0] += K * G_CHUNKS

                def spread(k, g):
                    return norm[:, k, bass.ds(g * G_GROUP, G_GROUP)].unsqueeze(2).to_broadcast([GP, G_GROUP, D])
                edges(0)
                edges(1)
                dve.wait_ge(deg_in, 32)
                step, k = stepper(count[0], 0, 0)
                step(V.tensor_scalar(deg[:, :, :], deg[:, :, :], 1.0, None, ALU.max))
                V.memset(newton[:, :, :], 0.0).then_inc(deg_made, 1)
                dve.wait_ge(rooted, 1)
                step(V.reciprocal(norm[:, :, :], root[:, :, :]))
                step(V.tensor_tensor(newton[:, :, :], norm[:, :, :], norm[:, :, :], ALU.mult))
                step(V.tensor_tensor(newton[:, :, :], newton[:, :, :], deg[:, :, :], ALU.mult))
                step(V.tensor_scalar(newton[:, :, :], newton[:, :, :], -0.5, 1.5, ALU.mult, ALU.add))
                step(V.tensor_tensor(norm[:, :, :], norm[:, :, :], newton[:, :, :], ALU.mult))
                count[0] += k[0]
                with dve.Fori(0, G_GROUPS) as g:
                    dve.wait_ge(group_in, 16 * g + 16)
                    V.tensor_tensor(yg[:, :, :], xg[:, :, :], spread(0, g), ALU.mult).then_inc(group_made, 1)
                for l in range(2):
                    edges(2 + l)
                    K = 3 if l == 0 else 7
                    with dve.Fori(0, G_GROUPS) as g:
                        step, k = stepper(count[0], K, g)
                        dve.wait_ge(group_in, 48 * g + (48 + 16 * G_GROUPS + 48 * l * G_GROUPS))
                        step(V.tensor_tensor(sg[:, :, :], sg[:, :, :], spread(1, g), ALU.mult))
                        V.tensor_tensor(uv[:, :, 0, :], sg[:, :, :], xg[:, :, :], ALU.add)
                        step(V.tensor_tensor(uv[:, :, 1, :], sg[:, :, :], xg[:, :, :], ALU.mult))
                        V.tensor_copy(mean[:, :], norm[:, 0, 0:G_GROUP]).then_inc(uv_made, 1)
                        dve.wait_ge(multiplied, g + (1 + l * G_GROUPS))
                        product = p_out[:, 0:G_GROUP * D].rearrange("p (t d) -> p t d", d=D)
                        if l == 0:
                            step(V.tensor_scalar(zg[:, :, :], product, 0.0, None, ALU.max))
                            V.tensor_tensor(yg[:, :, :], zg[:, :, :], spread(0, g), ALU.mult).then_inc(group_made, 1)
                        else:
                            across = lambda a: a[:, :].unsqueeze(2).to_broadcast([GP, G_GROUP, D])
                            step(V.tensor_tensor(zg[:, :, :], res[:, :, :], product, ALU.add))
                            step(V.tensor_reduce(mean[:, :], zg[:, :, :], AX.X, ALU.add))
                            step(V.tensor_scalar(mean[:, :], mean[:, :], 1.0 / D, None, ALU.mult))
                            V.tensor_tensor(zg[:, :, :], zg[:, :, :], across(mean), ALU.subtract).then_inc(centred, 1)
                            dve.wait_ge(squared, g + 1)
                            step(V.tensor_reduce(var[:, :], sq[:, :, :], AX.X, ALU.add))
                            V.tensor_copy(mean[:, :], norm[:, 0, 0:G_GROUP]).then_inc(var_made, 1)
                            dve.wait_ge(std_made, g + 1)
                            step(V.reciprocal(rstd[:, :], std[:, :]))
                            V.tensor_tensor(yg[:, :, :], zg[:, :, :], across(rstd), ALU.mult).then_inc(group_made, 1)
                        assert k[0] == K
                    count[0] += K * G_GROUPS


class Kept:

    def __init__(k, keep, ctx, weights):
        k.weights = weights
        k.ident, k.ones, k.eps, k.lane_no = (keep(n, [P, w], F32, ctx) for n, w in (("ident", P), ("ones", 1), ("eps", 1), ("lane_no", 1)))
        k.place, k.place16 = keep("place", [P, 3 * P], F32, ctx), keep("place16", [P, TILES], F16, ctx)
        k.wcat = keep("wcat", [2 * D, 2, D], F32, ctx)
        k.row_i = keep("row_i", [P, CHUNKS], I32, ctx)
        k.rel, k.src_lane, k.src_tile = (keep(n, [P, CHUNKS], F32, ctx) for n in ("rel", "src_lane", "src_tile"))
        k.deg, k.norm, k.norm2 = (keep(n, [P, TILES], F32, ctx) for n in ("deg", "norm", "norm2"))
        k.tally = keep("tally", [P, 4], F32, ctx)
        k.lane_r, k.rel_c = keep("lane_r", [P, RAWS], F32, ctx), keep("rel_c", [P, RAWS, 2], F16, ctx)
        k.deg_r, k.parts = keep("deg_r", [P, RAWS], F16, ctx), keep("parts", [P, RAWS, 3], F16, ctx)


INPUTS = ["x", "src", "dst", "L0_gnn_W1_1", "L0_gnn_W2_1", "L0_gnn_W1_2", "L0_gnn_W2_2"]


def build(nc, x, src, dst, weights, out, dram):
    tables = [dram["table0"], dram["table1"]]
    with ExitStack() as last:
        def keep(name, shape, dt=F32, stack=last):
            return stack.enter_context(nc.sbuf_tensor("k_" + name, shape, dt))
        flag, flag_i = keep("flag", [1, 1]), keep("flag_i", [1, 1], I32)
        with ExitStack() as ctx:
            k = Kept(keep, ctx, weights)
            place_edges(nc, src, dst, k)
            k.xh = keep("xh", [P, TILES, D], F32, ctx)
            sort_edges(nc, x, tables[0], k)
            layers(nc, x, out, tables, flag, k)
        with nc.semaphore("k_flag_made") as flag_made, nc.Block() as block:
            @block.vector
            def _(dve):
                nc.vector.tensor_copy(flag_i[:, :], flag[:, :]).then_inc(flag_made, 1)

        def if_needed(eng):
            return eng.If(eng.value_load(flag_i[0:1, 0:1]) > 0)
        general_path(nc, x, src, dst, weights, out, dram, if_needed)


def kernel(**inputs):
    import concourse.bacc as bacc
    from concourse.bass_utils import run_bass_kernel_spmd

    nc = bacc.Bacc("TRN2", target_bir_lowering=False, num_devices=1)
    arrays, aps = {}, {}
    for name in INPUTS:
        a = np.ascontiguousarray(inputs[name])
        arrays["in_" + name] = a
        aps[name] = nc.dram_tensor("in_" + name, a.shape, mybir.dt.from_np(a.dtype), kind="ExternalInput").ap()
    out = nc.dram_tensor("out", (N_NODES, D), F32, kind="ExternalOutput").ap()
    shapes = dict(G_DRAM, table0=(P, TILES * D), table1=(P, TILES * D))
    dram = {n: nc.dram_tensor(n, s, F32, kind="Internal").ap() for n, s in shapes.items()}
    build(nc, aps["x"], aps["src"], aps["dst"], [aps[n] for n in INPUTS[3:]], out, dram)
    r = run_bass_kernel_spmd(nc, [arrays], core_ids=[0])
    return r.results[0]["out"]
```

```python
from contextlib import ExitStack

import numpy as np

import concourse.bass as bass
from concourse import mybir

P = 128
N_NODES, D, N_EDGES = 50000, 64, 100000
EPS = 1e-5
F32 = mybir.dt.float32
I32 = mybir.dt.int32
ALU = mybir.AluOpType
ACT = mybir.ActivationFunctionType
AX = mybir.AxisListType

GN = 8
GROUP_NODES = GN * P
GROUPS = -(-N_NODES // GROUP_NODES)
TILES = GROUPS * GN
FULL_TILES = N_NODES // P
LAST_ROWS = N_NODES - FULL_TILES * P
CG = GN + 1
CHUNKS = GROUPS * CG
GROUP_SLOTS = CG * P
EB = 7
RUN = EB * P
EP = -(-N_EDGES // RUN)
LAST_RUN = N_EDGES - (EP - 1) * RUN
RAWS = EP * EB
RG = RAWS // GROUPS
HALO = P
WIN = 9
BACK = 4
SPAN = RG // 2 - 1 + WIN
GRID = (GROUPS - 1) * CG + SPAN
NO_EDGE = 65536
FAR = 10000.0
CAP = 2000.0
REACH = [[t for t in (j - 1, j, j + 1) if 0 <= t < GN] for j in range(CG)]
WIDTH = [P * len(r) for r in REACH]
SKIP = [P * (r[0] - (j - 1)) for j, r in enumerate(REACH)]
START = [sum(WIDTH[:j]) for j in range(CG)]
F16 = mybir.dt.float16
BF16 = mybir.dt.bfloat16
assert GROUPS % 2 == 1 and RAWS == GROUPS * RG and RG % 2 == 0 and LAST_RUN > HALO and TILES - FULL_TILES == 2


def runs(e, first, last):
    return e[first * RUN:last * RUN].rearrange("(p j) -> p j", j=RUN)


def place_edges(nc, src, dst, keepers):
    k = keepers
    with ExitStack() as ctx:
        def sb(name, shape, dt=F32):
            return ctx.enter_context(nc.sbuf_tensor("a_" + name, shape, dt))

        def sem(name):
            return ctx.enter_context(nc.semaphore("a_" + name))

        W = HALO + RUN
        s_i, d_i = sb("s_i", [EP, W], I32), sb("d_i", [EP, W + 1], I32)
        sf, df = sb("sf", [EP, W]), sb("df", [EP, W + 1])
        number = sb("number", [EP, W])
        is_self, step_up, drop, drop_no, last_drop = (sb(n, [EP, W]) for n in ("is_self", "step_up", "drop", "drop_no", "last_drop"))
        group_i, group = sb("group_i", [EP, RUN + 1], I32), sb("group", [EP, RUN + 1])
        kept_before, starts, base, behind, slot, keep, dev, degree, m1, m2, col_s, col_n = (
            sb(n, [EP, RUN]) for n in ("kept_before", "starts", "base", "behind", "slot", "keep", "dev", "degree", "m1", "m2", "col_s", "col_n"))
        place_i, target_i, lane_i, col_i, high_i, low_i = (sb(n, [EP, RUN], I32) for n in ("place_i", "target_i", "lane_i", "col_i", "high_i", "low_i"))
        lane, high, low = (sb(n, [EP, RUN]) for n in ("lane", "high", "low"))
        base_row, carry_row, carry = sb("base_row", [1, EP]), sb("carry_row", [1, EP + 1]), sb("carry", [EP, 1])
        win_s, win_n = sb("win_s", [P, RAWS]), sb("win_n", [P, RAWS])
        bank = [ctx.enter_context(nc.psum_tensor(f"a_bank{i}", [P, 512], F32)) for i in range(8)]
        padded, src_in, dst_in, w_in, consts, selected = sem("padded"), sem("src_in"), sem("dst_in"), sem("w_in"), sem("consts"), sem("selected")
        made, ints_made, floats_made = sem("made"), sem("ints_made"), sem("floats_made")
        base_made, base_up, carry_made, carry_down = sem("base_made"), sem("base_up"), sem("carry_made"), sem("carry_down")
        bytes_made, degree_made, columns_made, dev_made = (sem(n) for n in ("bytes_made", "degree_made", "columns_made", "dev_made"))
        turned, copied = sem("turned"), sem("copied")
        block = ctx.enter_context(nc.Block())

        OWN = slice(HALO, W)
        BEFORE = slice(HALO - 1, W - 1)
        by_raw = lambda a: a.rearrange("q (p b) -> q b p", b=EB)
        ARRAYS = [(high, k.parts[:, :, 0], bytes_made, 1), (low, k.parts[:, :, 1], bytes_made, 1), (degree, k.deg_r[:, :], degree_made, 1),
                  (lane, k.lane_r[:, :], floats_made, 2), (col_s, k.rel_c[:, :, 0], columns_made, 1), (col_n, k.rel_c[:, :, 1], columns_made, 2),
                  (dev, k.parts[:, :, 2], dev_made, 1)]
        BY_DVE = {4: win_s, 5: win_n}

        def halves(a):
            return [(bank[(2 * a + h) % 8], 4 * h, min(4, EB - 4 * h)) for h in range(2)]

        def load(eng, e, to, loaded):
            eng.dma_start(to[0:EP - 1, OWN], runs(e, 0, EP - 1)).then_inc(loaded, 16)
            eng.dma_start(to[EP - 1:EP, HALO:HALO + LAST_RUN], e[(EP - 1) * RUN:N_EDGES].unsqueeze(0)).then_inc(loaded, 16)
            eng.dma_start(to[1:EP, 0:HALO], runs(e, 0, EP - 1)[:, RUN - HALO:RUN]).then_inc(loaded, 16)

        @block.sync
        def _(sp):
            sp.wait_ge(padded, 1)
            load(sp, dst, d_i, dst_in)
            sp.dma_start(d_i[0:EP - 2, W:W + 1], runs(dst, 1, EP - 1)[:, 0:1], allow_slow_non_contiguous=True).then_inc(dst_in, 16)
            sp.dma_start(d_i[EP - 2:EP - 1, W:W + 1], dst[(EP - 1) * RUN:(EP - 1) * RUN + 1].unsqueeze(0)).then_inc(dst_in, 16)
            for l in range(2):
                for j in range(2):
                    sp.dma_start(k.wcat[j * D:(j + 1) * D, l, :], k.weights[2 * l + j]).then_inc(w_in, 16)
            sp.wait_ge(w_in, 64)

        @block.gpsimd
        def _(pool):
            G = nc.gpsimd
            free = dict(allow_small_or_imprecise_dtypes=True)
            G.memset(k.ident[:, :], 0.0).then_inc(selected, 1)
            G.iota(number[:, :], pattern=[[1, W]], base=1 - HALO, channel_multiplier=RUN, **free).then_inc(consts, 1)
            pool.wait_ge(selected, 1)
            G.affine_select(out=k.ident[:, :], in_=k.ident[:, :], compare_op=ALU.not_equal, fill=1.0,
                            base=0, pattern=[[-1, P]], channel_multiplier=1).then_inc(consts, 1)
            G.iota(win_s[:, :], pattern=[[CG, GROUPS], [1, RG // 2], [0, 2]], base=-BACK, channel_multiplier=0, **free).then_inc(consts, 1)
            G.iota(win_n[:, :], pattern=[[1, RAWS // 2], [0, 2]], base=-BACK, channel_multiplier=0, **free).then_inc(consts, 1)
            G.iota(k.place[:, :], pattern=[[1, 3 * P]], base=0, channel_multiplier=0, **free).then_inc(consts, 1)
            G.iota(k.place16[:, :], pattern=[[1, TILES]], base=0, channel_multiplier=0, **free).then_inc(consts, 1)
            G.iota(k.lane_no[:, :], pattern=[[1, 1]], base=0, channel_multiplier=1, **free).then_inc(consts, 1)
            G.iota(k.lanes[:, :, :], pattern=[[1, P], [0, RG]], base=0, channel_multiplier=0, **free)

        @block.tensor
        def _(pe):
            pe.wait_ge(consts, 7)
            for a, (array, _, ready, value) in enumerate(ARRAYS):
                if a == 3:
                    pe.wait_ge(base_made, 1)
                    nc.tensor.transpose(bank[6][0:1, 0:EP], base[:, RUN - 1:RUN], k.ident[0:EP, 0:EP]).then_inc(base_up, 1)
                    pe.wait_ge(carry_made, 1)
                    nc.tensor.matmul(bank[7][0:EP, 0:1], carry_row[0:1, 0:EP], k.ones[0:1, 0:1], start=True, stop=True).then_inc(carry_down, 1)
                pe.wait_ge(ready, value)
                if a >= 4:
                    pe.wait_ge(copied, a - 3)
                for b0, first, n in halves(a):
                    for b in range(n):
                        last = nc.tensor.transpose(b0[:, b * EP:(b + 1) * EP], array[:, (first + b) * P:(first + b + 1) * P],
                                                   k.ident[0:EP, 0:EP])
                last.then_inc(turned, 1)

        @block.scalar
        def _(act):
            act.wait_ge(padded, 2)
            load(act, src, s_i, src_in)
            act.wait_ge(src_in, 48)
            nc.scalar.activation(sf[:, :], s_i[:, :], ACT.Copy).then_inc(floats_made, 1)
            act.wait_ge(ints_made, 1)
            nc.scalar.activation(high[:, :], high_i[:, :], ACT.Copy)
            nc.scalar.activation(low[:, :], low_i[:, :], ACT.Copy).then_inc(bytes_made, 1)
            for a, (_, to, _, _) in enumerate(ARRAYS):
                if a == 3:
                    act.wait_ge(ints_made, 2)
                    nc.scalar.activation(lane[:, :], lane_i[:, :], ACT.Copy).then_inc(floats_made, 1)
                if a in BY_DVE:
                    continue
                act.wait_ge(turned, a + 1)
                for b0, first, n in halves(a):
                    last = nc.scalar.activation(by_raw(to)[:, first:first + n, :], b0[:, 0:n * EP].rearrange("q (b p) -> q b p", p=EP), ACT.Copy)
                last.then_inc(copied, 1)

        @block.vector
        def _(dve):
            V = nc.vector
            n = [0]

            def step(ins):
                n[0] += 1
                ins.then_inc(made, 1)
                dve.wait_ge(made, n[0])
            V.memset(d_i[:, :], NO_EDGE).then_inc(padded, 1)
            V.memset(s_i[:, :], 0).then_inc(padded, 1)
            V.memset(k.eps[:, :], EPS)
            V.memset(k.ones[:, :], 1.0)
            V.memset(k.tally[:, :], 0.0)
            V.memset(k.extreme[:, :], 0.0)
            V.memset(carry_row[:, :], 0.0)
            dve.wait_ge(dst_in, 80)
            V.tensor_copy(df[:, :], d_i[:, :])
            V.tensor_single_scalar(place_i[:, :], d_i[:, OWN], GROUP_NODES - 1, op=ALU.bitwise_and)
            step(V.tensor_single_scalar(group_i[:, :], d_i[:, HALO - 1:W], GROUP_NODES.bit_length() - 1, op=ALU.logical_shift_right))
            V.tensor_copy(group[:, :], group_i[:, :])
            V.tensor_tensor(step_up[:, :], df[:, 1:W + 1], df[:, 0:W], ALU.subtract)
            dve.wait_ge(src_in, 48)
            V.tensor_single_scalar(high_i[:, :], s_i[:, OWN], 8, op=ALU.logical_shift_right)
            V.tensor_single_scalar(low_i[:, :], s_i[:, OWN], 255, op=ALU.bitwise_and).then_inc(ints_made, 1)
            dve.wait_ge(consts, 7)
            dve.wait_ge(floats_made, 1)
            step(V.tensor_tensor(is_self[:, :], sf[:, :], df[:, 0:W], ALU.is_equal))
            step(V.scalar_tensor_tensor(drop[:, :], step_up[:, :], 0.0, is_self[:, :], ALU.not_equal, ALU.mult))
            step(V.tensor_tensor(drop_no[:, :], drop[:, :], number[:, :], ALU.mult))
            step(V.tensor_tensor_scan(last_drop[:, :], drop_no[:, :], drop_no[:, :], 0.0, ALU.max, ALU.max))
            step(V.tensor_tensor(m1[:, :], number[:, OWN], last_drop[:, BEFORE], ALU.subtract))
            step(V.tensor_tensor(degree[:, :], m1[:, :], drop[:, OWN], ALU.mult))
            V.tensor_scalar(degree[:, :], degree[:, :], CAP, None, ALU.min).then_inc(degree_made, 1)
            V.tensor_tensor(starts[:, :], group[:, 1:RUN + 1], group[:, 0:RUN], ALU.not_equal)
            step(V.scalar_tensor_tensor(kept_before[:, :], number[:, OWN], -1.0, df[:, OWN], ALU.add, ALU.subtract))
            step(V.tensor_tensor(starts[:, :], starts[:, :], kept_before[:, :], ALU.mult))
            V.tensor_tensor_scan(base[:, :], starts[:, :], starts[:, :], 0.0, ALU.max, ALU.max).then_inc(base_made, 1)
            V.tensor_reduce(k.extreme[0:EP, 0:1], degree[:, :], AX.X, ALU.max)
            dve.wait_ge(base_up, 1)
            step(V.tensor_copy(base_row[:, :], bank[6][0:1, 0:EP]))
            V.tensor_tensor_scan(carry_row[:, 1:EP + 1], base_row[:, :], base_row[:, :], 0.0, ALU.max, ALU.max).then_inc(carry_made, 1)
            step(V.scalar_tensor_tensor(keep[:, :], df[:, OWN], float(N_NODES), drop[:, OWN], ALU.is_lt, ALU.is_gt))
            V.tensor_tensor(m2[:, :], drop[:, OWN], df[:, OWN], ALU.mult)
            dve.wait_ge(carry_down, 1)
            step(V.tensor_copy(carry[:, :], bank[7][0:EP, 0:1]))
            step(V.scalar_tensor_tensor(behind[:, :], base[:, :], carry[:, :], kept_before[:, :], ALU.max, ALU.subtract))
            V.scalar_tensor_tensor(slot[:, :], group[:, 1:RUN + 1], float(GROUP_SLOTS), behind[:, :], ALU.mult, ALU.subtract)
            step(V.scalar_tensor_tensor(dev[:, :], behind[:, :], float(P), place_i[:, :], ALU.add, ALU.add))
            V.tensor_tensor(dev[:, :], dev[:, :], keep[:, :], ALU.mult)
            step(V.tensor_tensor(m1[:, :], slot[:, :], keep[:, :], ALU.mult))
            step(V.tensor_tensor(m1[:, :], m1[:, :], m2[:, :], ALU.add))
            step(V.tensor_scalar(target_i[:, :], m1[:, :], 0.0, float(NO_EDGE - 1), ALU.max, ALU.min))
            V.tensor_single_scalar(col_i[:, :], target_i[:, :], 7, op=ALU.logical_shift_right)
            V.tensor_single_scalar(lane_i[:, :], target_i[:, :], P - 1, op=ALU.bitwise_and).then_inc(ints_made, 1)
            dve.wait_ge(ints_made, 2)
            V.scalar_tensor_tensor(col_s[:, :], keep[:, :], -FAR, col_i[:, :], ALU.mult, ALU.add).then_inc(columns_made, 1)
            V.scalar_tensor_tensor(col_n[:, :], drop[:, OWN], -FAR, col_i[:, :], ALU.mult, ALU.add).then_inc(columns_made, 1)
            V.tensor_tensor(m2[:, :], dev[:, :], keep[:, :], ALU.subtract)
            V.tensor_scalar(dev[:, :], dev[:, :], CAP, -CAP, ALU.min, ALU.max).then_inc(dev_made, 1)
            dve.wait_ge(dev_made, 1)
            V.tensor_reduce(k.extreme[0:EP, 2:3], dev[:, :], AX.X, ALU.max)
            for a, win in BY_DVE.items():
                step(V.tensor_scalar(win[:, :], win[:, :], -FAR, None, ALU.add))
                dve.wait_ge(turned, a + 1)
                for b0, first, m in halves(a):
                    last = V.tensor_tensor(by_raw(ARRAYS[a][1])[:, first:first + m, :], b0[:, 0:m * EP].rearrange("q (b p) -> q b p", p=EP),
                                           by_raw(win)[:, first:first + m, :], ALU.subtract)
            V.tensor_reduce(k.extreme[0:EP, 3:4], m2[:, :], AX.X, ALU.min)
            V.tensor_reduce(k.extreme[0:EP, 1:2], step_up[:, OWN], AX.X, ALU.min)


def sort_edges(nc, x, table, keepers):
    k = keepers
    with ExitStack() as ctx:
        def sb(name, shape, dt=F32):
            return ctx.enter_context(nc.sbuf_tensor("b_" + name, shape, dt))

        def sem(name):
            return ctx.enter_context(nc.semaphore("b_" + name))

        PAIR = 2 * GN
        PAIRS = GROUPS // 2
        ACT_TILES = PAIR - 6
        grid = sb("grid", [P, 4, GRID])
        hot = sb("hot", [P, 2, P, RG], F16)
        hot_col = sb("hot_col", [P, 2, RG, 2, WIN], F16)
        spread = sb("spread", [P, 2, RG, 4, WIN], F16)
        nil = sb("nil", [P, P], F16)
        src_f, src_i, slane_i, stile_i = sb("src_f", [P, CHUNKS]), sb("src_i", [P, CHUNKS], I32), sb("slane_i", [P, CHUNKS], I32), sb("stile_i", [P, CHUNKS], I32)
        empty, filled, here = sb("empty", [P, CHUNKS]), sb("filled", [P, CHUNKS]), sb("here", [P, TILES])
        root, square = sb("root", [P, TILES]), sb("square", [P, TILES])
        y = sb("y", [P, 2, PAIR, D])
        END = (PAIRS - 1) * PAIR
        y_end = sb("y_end", [P, TILES - END, D])
        whole_bank = [ctx.enter_context(nc.psum_tensor(f"b_bank{i}", [P, 512], F32)) for i in range(2)]
        bank = [b[:, 0:4 * SPAN].rearrange("p (a c) -> p a c", a=4) for b in whole_bank]
        padded, nil_made = sem("padded"), sem("nil_made")
        hots_made, columns_made, spread_made, placed, added, made = sem("hots_made"), sem("columns_made"), sem("spread_made"), sem("placed"), sem("added"), sem("made")
        deg_made, root_made, norm_step, norm_made, scaled = sem("deg_made"), sem("root_made"), sem("norm_step"), sem("norm_made"), sem("scaled")
        src_made, scaled_too, end_scaled, end_out = sem("src_made"), sem("scaled_too"), sem("end_scaled"), sem("end_out")
        x_in, out_sem = [sem(f"x_in{j}") for j in range(2)], [sem(f"table_out{j}") for j in range(2)]
        block = ctx.enter_context(nc.Block())
        x_full = x[0:FULL_TILES * P, :].rearrange("(t p) d -> p t d", p=P)

        def rounds(eng, body):
            with eng.Fori(0, PAIRS // 2) as i:
                for j in range(4):
                    body(j % 2, 4 * i + j)
            body(0, GROUPS - 1)

        @block.sync
        def _(sp):
            sp.wait_ge(padded, 1)

            def load(j, p):
                sp.dma_start(k.xh[:, bass.ds(p * PAIR, PAIR), :], x_full[:, bass.ds(p * PAIR, PAIR), :]).then_inc(x_in[j], 16)
            for j in range(2):
                load(j, j)
            with sp.Fori(1, PAIRS // 2) as i:
                for j in range(2):
                    sp.wait_ge(x_in[j], 16 * i)
                    sp.nop(nofuse=True)
                    load(j, 2 * i + j)
            sp.wait_ge(x_in[0], 8 * PAIRS)
            sp.dma_start(k.xh[:, PAIR * PAIRS:FULL_TILES, :], x_full[:, PAIR * PAIRS:FULL_TILES, :]).then_inc(x_in[0], 16)
            sp.dma_start(k.xh[0:LAST_ROWS, FULL_TILES, :], x[FULL_TILES * P:N_NODES, :]).then_inc(x_in[0], 16)
            sp.wait_ge(end_scaled, 1)
            sp.dma_start(table[:, END * D:TILES * D], y_end[:, :, :].rearrange("p t d -> p (t d)")).then_inc(end_out, 16)
            sp.wait_ge(end_out, 16)

        @block.gpsimd
        def _(pool):
            nc.gpsimd.memset(nil[:, :], 0.0).then_inc(nil_made, 1)

            def body(j, g):
                pool.wait_ge(placed, g + 1)
                pool.nop(nofuse=True)
                part = bass.ds(g * RG, RG)
                pool.wait_ge(columns_made, g + 1)
                pool.nop(nofuse=True)
                nc.gpsimd.tensor_tensor(spread[:, j, :, 0:3, :], hot_col[:, j, :, 0, :].unsqueeze(2).to_broadcast([P, RG, 3, WIN]),
                                        k.parts[:, part, :].unsqueeze(3).to_broadcast([P, RG, 3, WIN]), ALU.mult)
                nc.gpsimd.tensor_tensor(spread[:, j, :, 3, :], hot_col[:, j, :, 1, :], k.deg_r[:, part].unsqueeze(2).to_broadcast([P, RG, WIN]),
                                        ALU.mult).then_inc(spread_made, 1)
            rounds(pool, body)

        @block.tensor
        def _(pe):
            pe.wait_ge(nil_made, 1)
            nil_cols = nil[:, 0:4 * SPAN].rearrange("p (a b) -> p a b", a=4)
            for j in range(2):
                nc.tensor.matmul(bank[j][:, :, :], nil[:, :], nil_cols, start=True, stop=True).then_inc(placed, 1)

            def body(j, g):
                pe.wait_ge(added, g + 1)
                nc.tensor.matmul(bank[j][:, :, :], nil[:, :], nil_cols, start=True, stop=False, skip_group_check=True)
                pe.wait_ge(hots_made, g + 1)
                pe.wait_ge(spread_made, g + 1)
                for r in range(RG):
                    last = nc.tensor.matmul(bank[j][:, :, r // 2:r // 2 + WIN], hot[:, j, :, r], spread[:, j, r],
                                            start=False, stop=r == RG - 1, skip_group_check=True)
                last.then_inc(placed, 1)
            rounds(pe, body)

        @block.scalar
        def _(act):
            A = nc.scalar.activation

            def roots(p, tiles):
                act.wait_ge(deg_made, p + 1)
                act.nop(nofuse=True)
                A(root[:, tiles], k.deg[:, tiles], ACT.Sqrt).then_inc(root_made, 1)

            def rows(j, p):
                act.wait_ge(norm_made, p + 1)
                act.wait_ge(x_in[j], (p - j) * 8 + 16)
                if not isinstance(p, int) or p > 1:
                    act.wait_ge(out_sem[j], (p - j) * 8)
                act.nop(nofuse=True)
                for t in range(ACT_TILES):
                    last = A(y[:, j, t, :], k.xh[:, bass.ds(p * PAIR + t, 1), :].rearrange("p t d -> p (t d)"), ACT.Copy,
                             scale=k.norm[:, bass.ds(p * PAIR + t, 1)])
                last.then_inc(scaled, 1)

            def store(j, p):
                act.wait_ge(scaled, p + 1)
                act.wait_ge(scaled_too, p + 1)
                act.dma_start(table[:, bass.ds(p * (PAIR * D), PAIR * D)], y[:, j].rearrange("p t d -> p (t d)")).then_inc(out_sem[j], 16)

            def pair(p):
                return bass.ds(p * PAIR, PAIR)

            roots(0, pair(0))
            for j in range(2):
                roots(j + 1, pair(j + 1))
                rows(j, j)
                store(j, j)
            with act.Fori(1, PAIRS // 2 - 1) as i:
                for j in range(2):
                    roots(2 * i + (j + 1), pair(2 * i + (j + 1)))
                    rows(j, 2 * i + j)
                    store(j, 2 * i + j)
            roots(PAIRS - 1, slice(END, TILES))
            rows(0, PAIRS - 2)
            store(0, PAIRS - 2)
            act.wait_ge(src_made, 1)
            A(k.src_tile[:, :], stile_i[:, :], ACT.Copy)
            act.wait_ge(out_sem[0], 8 * PAIRS)
            act.wait_ge(out_sem[1], 8 * PAIRS - 16)

        @block.vector
        def _(dve):
            V = nc.vector
            V.memset(k.xh[:, FULL_TILES:TILES, :], 0.0).then_inc(padded, 1)
            V.memset(here[:, :], 0.0).then_inc(added, 1)
            V.memset(grid[:, :, :], 0.0).then_inc(added, 1)
            n = [0]

            def step(ins):
                n[0] += 1
                ins.then_inc(made, 1)
                dve.wait_ge(made, n[0])

            def columns(j, g):
                if not isinstance(g, int) or g > 1:
                    dve.wait_ge(spread_made, g - 1)
                V.tensor_tensor(hot_col[:, j], k.place16[:, 0:WIN].unsqueeze(1).unsqueeze(1).to_broadcast([P, RG, 2, WIN]),
                                k.rel_c[:, bass.ds(g * RG, RG), :].unsqueeze(3).to_broadcast([P, RG, 2, WIN]), ALU.is_equal).then_inc(columns_made, 1)

            def hots(j, g, half):
                if half == 0:
                    dve.wait_ge(placed, g + 1)
                part = slice(half * (P // 2), (half + 1) * (P // 2))
                last = V.tensor_tensor(hot[:, j, part, :], k.lanes[:, part, :],
                                       k.lane_r[:, bass.ds(g * RG, RG)].unsqueeze(1).to_broadcast([P, P // 2, RG]), ALU.is_equal)
                if half == 1:
                    last.then_inc(hots_made, 1)

            def add(j, g):
                dve.wait_ge(placed, g + 3)
                dve.wait_ge(added, g + 2)
                s, m = grid[:, 0:3, bass.ds(g * CG, SPAN)], grid[:, 3, bass.ds(g * GN, SPAN)]
                V.tensor_tensor(s, s, bank[j][:, 0:3, :], ALU.add)
                V.tensor_tensor(m, m, bank[j][:, 3, :], ALU.add).then_inc(added, 1)

            def norms(p, tiles):
                r, d, q = k.norm[:, tiles], k.deg[:, tiles], square[:, tiles]

                def wait(m):
                    dve.wait_ge(norm_step, p * 5 + m)

                def start():
                    dve.wait_ge(root_made, p + 1)
                    dve.nop(nofuse=True)
                    V.reciprocal(r, root[:, tiles]).then_inc(norm_step, 1)

                def squared():
                    wait(1)
                    V.tensor_tensor(q, r, r, ALU.mult).then_inc(norm_step, 1)

                def times_degree():
                    wait(2)
                    V.tensor_tensor(q, q, d, ALU.mult).then_inc(norm_step, 1)

                def halved():
                    wait(3)
                    V.tensor_scalar(q, q, -0.5, 1.5, ALU.mult, ALU.add).then_inc(norm_step, 1)

                def finished():
                    wait(4)
                    V.tensor_tensor(r, r, q, ALU.mult).then_inc(norm_step, 1)
                    wait(5)
                    V.tensor_tensor(k.norm2[:, tiles], r, r, ALU.mult).then_inc(norm_made, 1)
                return start, squared, times_degree, halved, finished

            nothing = [lambda: None] * 5

            def pair(p):
                return bass.ds(p * PAIR, PAIR)

            def rows(j, p):
                dve.wait_ge(norm_step, p * 5 + 5)
                dve.wait_ge(x_in[j], (p - j) * 8 + 16)
                if not isinstance(p, int) or p > 1:
                    dve.wait_ge(out_sem[j], (p - j) * 8)
                tiles = bass.ds(p * PAIR + ACT_TILES, PAIR - ACT_TILES)
                V.tensor_tensor(y[:, j, ACT_TILES:PAIR], k.xh[:, tiles, :], k.norm[:, tiles].unsqueeze(2).to_broadcast([P, PAIR - ACT_TILES, D]),
                                ALU.mult).then_inc(scaled_too, 1)

            def body(i, p, late, j=0):
                start, squared = (nothing if p is None else norms(p, pair(p)))[:2]
                times_degree, halved, finished = (nothing if late is None else norms(late, pair(late)))[2:]
                hots(1, 2 * i + 1, 0)
                times_degree()
                hots(1, 2 * i + 1, 1)
                halved()
                add(0, 2 * i)
                finished()
                columns(0, 2 * i + 2)
                if p is not None:
                    dve.wait_ge(added, 2 * i + 3)
                    V.tensor_scalar(k.deg[:, pair(p)], grid[:, 3, bass.ds(p * PAIR + BACK, PAIR)], 1.0, None, ALU.max).then_inc(deg_made, 1)
                hots(0, 2 * i + 2, 0)
                hots(0, 2 * i + 2, 1)
                if late is not None:
                    rows(j, late)
                start()
                add(1, 2 * i + 1)
                squared()
                if not isinstance(i, int) or i < PAIRS - 1:
                    columns(1, 2 * i + 3)
            columns(0, 0)
            for c, (limit, op) in enumerate(((float(HALO), ALU.is_gt), (0.0, ALU.is_lt), (2.0 * P, ALU.is_gt), (0.0, ALU.is_lt))):
                last = V.tensor_scalar(k.extreme[:, c:c + 1], k.extreme[:, c:c + 1], limit, None, op)
            step(last)
            V.tensor_reduce(k.tally[:, 0:1], k.extreme[:, :], AX.X, ALU.add)
            hots(0, 0, 0)
            hots(0, 0, 1)
            columns(1, 1)
            body(0, None, None)
            body(1, 0, None)
            body(2, 1, 0)
            with dve.Fori(0, PAIRS // 2 - 2) as i:
                for n2 in range(3, 5):
                    body(2 * i + n2, 2 * i + (n2 - 1), 2 * i + (n2 - 2), n2 % 2)
            body(PAIRS - 1, PAIRS - 2, PAIRS - 3, (PAIRS - 3) % 2)
            add(0, GROUPS - 1)
            for norm_op in norms(PAIRS - 2, pair(PAIRS - 2))[2:]:
                norm_op()
            rows(0, PAIRS - 2)
            slots, nodes = slice(BACK, BACK + CHUNKS), slice(BACK, BACK + TILES)
            end = slice(END, TILES)
            dve.wait_ge(added, GROUPS + 2)
            V.tensor_scalar(k.deg[:, end], grid[:, 3, BACK + END:BACK + TILES], 1.0, None, ALU.max).then_inc(deg_made, 1)
            last_norms = norms(PAIRS - 1, end)
            step(V.scalar_tensor_tensor(src_f[:, :], grid[:, 0, slots], 256.0, grid[:, 1, slots], ALU.mult, ALU.add))
            step(V.tensor_scalar(src_i[:, :], src_f[:, :], 0.0, float(N_NODES - 1), ALU.max, ALU.min))
            V.tensor_single_scalar(slane_i[:, :], src_i[:, :], P - 1, op=ALU.bitwise_and)
            V.tensor_single_scalar(stile_i[:, :], src_i[:, :], 7, op=ALU.logical_shift_right).then_inc(src_made, 1)
            V.tensor_scalar(empty[:, :], grid[:, 2, slots], 0.0, FAR, ALU.is_equal, ALU.mult)
            for norm_op in last_norms:
                norm_op()
            dve.wait_ge(norm_made, PAIRS)
            dve.wait_ge(x_in[0], 8 * PAIRS + 32)
            dve.wait_ge(x_in[1], 8 * PAIRS)
            V.tensor_tensor(y_end[:, :, :], k.xh[:, END:TILES, :], k.norm[:, END:TILES].unsqueeze(2).to_broadcast([P, TILES - END, D]),
                            ALU.mult).then_inc(end_scaled, 1)
            dve.wait_ge(src_made, 1)
            V.scalar_tensor_tensor(k.row_i[:, :], slane_i[:, :], float(TILES), stile_i[:, :], ALU.mult, ALU.add)
            V.scalar_tensor_tensor(k.rel[:, :], grid[:, 2, slots], k.lane_no[:, :], empty[:, :], ALU.add, ALU.add)
            V.tensor_tensor(k.src_lane[:, :], slane_i[:, :], empty[:, :], ALU.add)
            V.tensor_scalar(here[:, :], grid[:, 3, nodes], 1.0, None, ALU.is_ge)
            step(V.tensor_scalar(filled[:, :], grid[:, 2, slots], 1.0, None, ALU.is_ge))
            V.tensor_reduce(k.tally[:, 1:2], filled[:, :], AX.X, ALU.add)
            V.tensor_reduce(k.tally[:, 2:3], here[:, :], AX.X, ALU.add)


HIST = 3
PARTS = 3
BATCH = 3
NB = CG // BATCH


def layer(nc, l, x, out, tables, flag, keepers):
    k = keepers
    with ExitStack() as ctx:
        def sb(name, shape, dt=F32):
            return ctx.enter_context(nc.sbuf_tensor(f"c{l}_" + name, shape, dt))

        def sem(name):
            return ctx.enter_context(nc.semaphore(f"c{l}_" + name))

        def ps(name, shape):
            return ctx.enter_context(nc.psum_tensor(f"c{l}_" + name, shape, F32))

        parts, dt = ((1, F32), (PARTS, BF16))[l]
        counted_here = (range(HIST), range(HIST, CG))[l]
        row_s = sb("row_s", [P, 2, CG], I32)
        rows = sb("rows", [P, 2, CG, parts, D], dt)
        sel = sb("sel", [P, 2, sum(WIDTH)], dt)
        place = (k.place, k.place16)[l]
        uv = sb("uv", [P, 2, GN, 2, D])
        scaled, own, sums = sb("scaled", [P, GN, D]), sb("own", [P, GN, D]), sb("sums", [P, GN, D])
        uvt = sb("uvt", [P, GN, P])
        hot_l, hot_t = sb("hot_l", [P, len(counted_here), P], F16), sb("hot_t", [P, len(counted_here), TILES], F16)
        nil = sb("nil", [P, TILES], F16)
        if l == 0:
            yf, rest = sb("yf", [P, GN, D]), sb("rest", [P, GN, D])
            y = sb("y", [P, 2, GN, PARTS, D], BF16)
        else:
            y = sb("y", [P, 2, GN, D])
            res = sb("res", [P, 2, GN, D])
            z, sq = sb("z", [P, 2, GN, D]), sb("sq", [P, GN, D])
            total, var, std, rstd = (sb(n, [P, 2, GN]) for n in ("total", "var", "std", "rstd"))
            differs, totals, bad = sb("differs", [P, TILES]), sb("totals", [1, 4]), sb("bad", [1, 4])
            p_tally = ps("tally", [1, 512])
        p_sum, p_out = [ps(f"sum{i}", [P, GN, D]) for i in range(2)], [ps(f"out{i}", [P, GN, D]) for i in range(2)]
        p_turn = [ps(f"turn{i}", [P, 4, P]) for i in range(2)]
        staged, sel_made, summed, own_made, scaled_made, sums_made, uv_made, turned, uvt_made, multiplied = (sem(n) for n in (
            "staged", "sel_made", "summed", "own_made", "scaled_made", "sums_made", "uv_made", "turned", "uvt_made", "multiplied"))
        yf_made, hi_made, rest_made, mid_made, y_made = (sem(n) for n in ("yf_made", "hi_made", "rest_made", "mid_made", "y_made"))
        z_made, total_made, centred, squared, var_made, std_made, rstd_made = (sem(n) for n in (
            "z_made", "total_made", "centred", "squared", "var_made", "std_made", "rstd_made"))
        hots_made, counted, nil_made, cleared = sem("hots_made"), sem("counted"), sem("nil_made"), sem("cleared")
        tally_made, tallied, verdict_step = sem("tally_made"), sem("tallied"), sem("verdict_step")
        gathered = [[sem(f"gathered{j}{b}") for b in range(NB)] for j in range(2)]
        stored, res_in = [sem(f"stored{j}") for j in range(2)], [sem(f"res_in{j}") for j in range(2)]
        block = ctx.enter_context(nc.Block())
        x_full = x[0:FULL_TILES * P, :].rearrange("(t p) d -> p t d", p=P)
        out_full = out[0:FULL_TILES * P, :].rearrange("(t p) d -> p t d", p=P)
        PAST = FULL_TILES - (GROUPS - 1) * GN

        def done(eng, s, v):
            if not (isinstance(v, int) and v <= 0):
                eng.wait_ge(s, v)

        def moved(eng, s, g, j, n=16):
            if not isinstance(g, int) or g >= 0:
                eng.wait_ge(s, (g - j) * (n // 2) + n)

        def steps(eng, body):
            for t in range(4):
                body(t, t % 2)
            with eng.Fori(2, GROUPS // 2) as i:
                for j in range(2):
                    body(2 * i + j, j)
            for t in range(GROUPS - 1, GROUPS + 3):
                body(t, t % 2)

        def live(t, back):
            return not isinstance(t, int) or 0 <= t - back < GROUPS

        def final(g):
            return isinstance(g, int) and g == GROUPS - 1

        def group(g):
            return bass.ds(g * GN, GN)

        @block.sync
        def _(sp):
            if l == 1:
                sp.wait_ge(cleared, 1)

            def body(t, j):
                if live(t, 3):
                    g, b = t - 3, 1 - j
                    sp.wait_ge(y_made, g + 1)
                    if l == 0:
                        n = GN * PARTS * D
                        sp.dma_start(tables[1][:, bass.ds(g * n, n)], y[:, b].rearrange("p t q d -> p (t q d)")).then_inc(stored[b], 16)
                    elif final(g):
                        sp.dma_start(out_full[:, g * GN:FULL_TILES, :], y[:, b, 0:PAST]).then_inc(stored[b], 16)
                        sp.dma_start(out[FULL_TILES * P:N_NODES, :], y[0:LAST_ROWS, b, PAST]).then_inc(stored[b], 16)
                    else:
                        sp.dma_start(out_full[:, group(g), :], y[:, b]).then_inc(stored[b], 16)
                if l == 1 and live(t, 0):
                    done(sp, z_made, t - 1)
                    if not isinstance(t, int):
                        sp.nop(nofuse=True)
                    if isinstance(t, int) and t == GROUPS - 1:
                        sp.dma_start(res[:, j, 0:PAST], x_full[:, t * GN:FULL_TILES, :]).then_inc(res_in[j], 16)
                        sp.dma_start(res[0:LAST_ROWS, j, PAST], x[FULL_TILES * P:N_NODES, :]).then_inc(res_in[j], 16)
                    else:
                        sp.dma_start(res[:, j], x_full[:, group(t), :]).then_inc(res_in[j], 16)
            steps(sp, body)
            sp.wait_ge(stored[0], 16 * (GROUPS // 2 + 1 + l))
            sp.wait_ge(stored[1], 16 * (GROUPS // 2))

        @block.gpsimd
        def _(pool):
            table = tables[l].rearrange("p (t d) -> (p t) d", d=parts * D)
            nc.gpsimd.memset(nil[:, :], 0.0).then_inc(nil_made, 1)

            def body(t, j):
                if live(t, 0):
                    pool.wait_ge(staged, t + 1)
                    pool.nop(nofuse=True)
                    done(pool, summed, t - 1)
                    pool.nop(nofuse=True)
                    for c in range(CG):
                        nc.gpsimd.indirect_dma_start(out=rows[:, j, c].rearrange("p q d -> p (q d)"), out_offset=None, in_=table,
                                                     in_offset=bass.IndirectOffsetOnAxis(ap=row_s[:, j, c:c + 1], axis=0)
                                                     ).then_inc(gathered[j][c // BATCH], 16)
            steps(pool, body)

        @block.tensor
        def _(pe):
            pe.wait_ge(nil_made, 1)
            if l == 0:
                nc.tensor.matmul(k.p_count[:, 0:TILES], nil[:, 0:P], nil[:, :], start=True, stop=False, skip_group_check=True)

            def add_up(t, j, b):
                if b == 0:
                    done(pe, scaled_made, t - 1)
                pe.wait_ge(sel_made, t * NB + (b + 1))
                moved(pe, gathered[j][b], t, j, 16 * BATCH)
                for c in range(BATCH * b, BATCH * (b + 1)):
                    for n, tile in enumerate(REACH[c]):
                        for q in range(parts):
                            last = nc.tensor.matmul(p_sum[j][:, tile, :], sel[:, j, START[c] + n * P:START[c] + (n + 1) * P], rows[:, j, c, q],
                                                    start=c == 0 and n == 0 and q == 0, stop=c == CG - 1, skip_group_check=True)
                if b == NB - 1:
                    last.then_inc(summed, 1)

            def body(t, j):
                if live(t, 2):
                    pe.wait_ge(uvt_made, t - 1)
                    done(pe, z_made if l else hi_made, t - 3)
                    for tile in range(GN):
                        last = nc.tensor.matmul(p_out[j][:, tile, :], uvt[:, tile, :], k.wcat[:, l, :], start=True, stop=True)
                    last.then_inc(multiplied, 1)
                if live(t, 0):
                    add_up(t, j, 0)
                    pe.wait_ge(hots_made, t + 1)
                    for c in range(len(counted_here)):
                        last = nc.tensor.matmul(k.p_count[:, 0:TILES], hot_l[:, c], hot_t[:, c], start=False, stop=False, skip_group_check=True)
                    last.then_inc(counted, 1)
                if live(t, 1):
                    pe.wait_ge(uv_made, t)
                    for tile in range(GN):
                        last = nc.tensor.transpose(p_turn[tile // 4][:, tile % 4, :], uv[:, 1 - j, tile].rearrange("p a d -> p (a d)"), k.ident[:, :])
                    last.then_inc(turned, 1)
                if live(t, 0):
                    for b in range(1, NB):
                        add_up(t, j, b)
                if l == 1 and isinstance(t, int) and t == GROUPS - 1:
                    nc.tensor.matmul(k.p_count[:, 0:TILES], nil[:, 0:P], nil[:, :], start=False, stop=True, skip_group_check=True).then_inc(counted, 1)
                if l == 1 and isinstance(t, int) and t == GROUPS:
                    pe.wait_ge(tally_made, 1)
                    nc.tensor.matmul(p_tally[0:1, 0:4], k.ones[:, :], k.tally[:, :], start=True, stop=True).then_inc(tallied, 1)
            steps(pe, body)

        @block.scalar
        def _(act):
            A = nc.scalar.activation

            def tiles(a, g, n):
                return a[:, bass.ds(g * GN + n, 1)]

            def finish(t, j):
                g, b = t - 3, 1 - j
                if l == 0:
                    act.wait_ge(rest_made, g + 1)
                    act.nop(nofuse=True)
                    A(y[:, b, :, 1, :], rest[:, :, :], ACT.Copy).then_inc(mid_made, 1)
                else:
                    act.wait_ge(centred, g + 1)
                    A(sq[:, :, :], z[:, b], ACT.Square).then_inc(squared, 1)

            def body(t, j):
                if live(t, 3):
                    finish(t, j)
                if live(t, 1):
                    g = t - 1
                    done(act, sums_made, g)
                    if not isinstance(g, int):
                        act.nop(nofuse=True)
                    for n in range(GN):
                        last = A(own[:, n, :], k.xh[:, bass.ds(g * GN + n, 1), :].rearrange("p t d -> p (t d)"), ACT.Copy, scale=tiles(k.norm2, g, n))
                    last.then_inc(own_made, 1)
                if l == 1 and live(t, 3):
                    act.wait_ge(var_made, t - 2)
                    A(std[:, 1 - j], var[:, 1 - j], ACT.Sqrt, bias=k.eps[:, :], scale=1.0 / D).then_inc(std_made, 1)
                if live(t, 1) and not final(g):
                    act.wait_ge(summed, g + 1)
                    act.nop(nofuse=True)
                    for n in range(GN):
                        last = A(scaled[:, n, :], p_sum[1 - j][:, n, :], ACT.Copy, scale=tiles(k.norm, g, n))
                    last.then_inc(scaled_made, 1)
                if l == 0 and live(t, 2):
                    g = t - 2
                    act.wait_ge(multiplied, g + 1)
                    act.nop(nofuse=True)
                    for n in range(GN):
                        last = A(yf[:, n, :], p_out[j][:, n, :], ACT.Relu, scale=tiles(k.norm, g, n))
                    last.then_inc(yf_made, 1)
                    A(k.xh[:, group(g), :], p_out[j][:, :, :], ACT.Relu)
                    moved(act, stored[j], g - 2, j)
                    act.wait_ge(yf_made, g + 1)
                    act.nop(nofuse=True)
                    A(y[:, j, :, 0, :], yf[:, :, :], ACT.Copy).then_inc(hi_made, 1)
                if l == 1 and live(t, 3) and not final(t - 3):
                    g, b = t - 3, 1 - j
                    moved(act, stored[b], g - 2, b)
                    act.nop(nofuse=True)
                    act.wait_ge(rstd_made, g + 1)
                    act.nop(nofuse=True)
                    for n in range(GN):
                        last = A(y[:, b, n, :], z[:, b, n, :], ACT.Copy, scale=rstd[:, b, n:n + 1])
                    last.then_inc(y_made, 1)
                if live(t, 1):
                    act.wait_ge(turned, t)
                    for h in range(2):
                        last = A(uvt[:, 4 * h:4 * h + 4, :], p_turn[h][:, :, :], ACT.Copy)
                    last.then_inc(uvt_made, 1)
            steps(act, body)

        @block.vector
        def _(dve):
            V = nc.vector
            if l == 1:
                V.memset(res[:, :, :, :], 0.0).then_inc(cleared, 1)

            def stage(t, j):
                for b in range(NB):
                    moved(dve, gathered[j][b], t - 2, j, 16 * BATCH)
                dve.nop(nofuse=True)
                V.tensor_copy(row_s[:, j, :], k.row_i[:, bass.ds(t * CG, CG)]).then_inc(staged, 1)

            def select(t, j, chunks):
                if chunks[0] == 0 and live(t, 0):
                    done(dve, summed, t - 1)
                for c in chunks:
                    if live(t, 0):
                        last = V.tensor_scalar(sel[:, j, START[c]:START[c] + WIDTH[c]], place[:, SKIP[c]:SKIP[c] + WIDTH[c]],
                                               k.rel[:, bass.ds(t * CG + c, 1)], None, ALU.is_equal)
                        if c % BATCH == BATCH - 1:
                            last.then_inc(sel_made, 1)

            def count(t, part):
                if live(t, 0):
                    if part[0] == 0:
                        done(dve, counted, t)
                    for n in part:
                        c = counted_here[n]
                        V.tensor_scalar(hot_l[:, n], k.place16[:, 0:P], k.src_lane[:, bass.ds(t * CG + c, 1)], None, ALU.is_equal)
                        last = V.tensor_scalar(hot_t[:, n], k.place16[:, :], k.src_tile[:, bass.ds(t * CG + c, 1)], None, ALU.is_equal)
                    if part[-1] == len(counted_here) - 1:
                        last.then_inc(hots_made, 1)

            stage(0, 0)
            select(0, 0, range(CG))
            half = len(counted_here) // 2

            def verdict():
                dve.wait_ge(counted, GROUPS + 1)
                V.scalar_tensor_tensor(differs[:, :], k.p_count[:, 0:TILES], 1.0, k.deg[:, :], ALU.add, ALU.not_equal).then_inc(verdict_step, 1)
                dve.wait_ge(verdict_step, 1)
                V.tensor_reduce(k.tally[:, 3:4], differs[:, :], AX.X, ALU.add).then_inc(tally_made, 1)

            def verdict_end():
                dve.wait_ge(tallied, 1)
                V.tensor_copy(totals[:, :], p_tally[0:1, 0:4]).then_inc(verdict_step, 1)
                dve.wait_ge(verdict_step, 2)
                for c, want in enumerate((0, N_EDGES - N_NODES, N_NODES, 0)):
                    last = V.tensor_scalar(bad[:, c:c + 1], totals[:, c:c + 1], float(want), None, ALU.not_equal)
                last.then_inc(verdict_step, 1)
                dve.wait_ge(verdict_step, 3)
                V.tensor_reduce(totals[:, 0:1], bad[:, :], AX.X, ALU.add).then_inc(verdict_step, 1)
                dve.wait_ge(verdict_step, 4)
                V.tensor_copy(flag[:, :], totals[:, 0:1])

            def body(t, j):
                if l == 1 and isinstance(t, int) and t == GROUPS:
                    verdict()
                if l == 1 and isinstance(t, int) and t == GROUPS + 1:
                    verdict_end()
                count(t, range(half))
                if live(t, 3):
                    g, b = t - 3, 1 - j
                    if l == 0:
                        dve.wait_ge(mid_made, g + 1)
                        V.tensor_tensor(y[:, b, :, 2, :], rest[:, :, :], y[:, b, :, 1, :], ALU.subtract).then_inc(y_made, 1)
                    else:
                        dve.wait_ge(squared, g + 1)
                        dve.nop(nofuse=True)
                        V.tensor_reduce(var[:, b], sq[:, :, :], AX.X, ALU.add).then_inc(var_made, 1)
                if live(t, -1):
                    stage(t + 1, 1 - j)
                count(t, range(half, len(counted_here)))
                select(t + 1, 1 - j, (0,))
                if l == 1 and live(t, 3):
                    dve.wait_ge(std_made, t - 2)
                    V.reciprocal(rstd[:, 1 - j], std[:, 1 - j]).then_inc(rstd_made, 1)
                    if final(t - 3):
                        dve.wait_ge(rstd_made, GROUPS)
                        moved(dve, stored[1 - j], t - 5, 1 - j)
                        V.tensor_tensor(y[:, 1 - j], z[:, 1 - j], rstd[:, 1 - j].unsqueeze(2).to_broadcast([P, GN, D]), ALU.mult).then_inc(y_made, 1)
                select(t + 1, 1 - j, (1, 2, 3))
                if live(t, 1):
                    g = t - 1
                    h = k.xh[:, group(g), :]
                    if final(g):
                        dve.wait_ge(summed, g + 1)
                        V.tensor_tensor(scaled[:, :, :], p_sum[1 - j][:, :, :], k.norm[:, group(g)].unsqueeze(2).to_broadcast([P, GN, D]),
                                        ALU.mult).then_inc(scaled_made, 1)
                    dve.wait_ge(own_made, g + 1)
                    dve.wait_ge(scaled_made, g + 1)
                    V.tensor_tensor(sums[:, :, :], scaled[:, :, :], own[:, :, :], ALU.add).then_inc(sums_made, 1)
                select(t + 1, 1 - j, (4,))
                if live(t, 1):
                    done(dve, turned, g - 1)
                    dve.wait_ge(sums_made, g + 1)
                    V.tensor_tensor(uv[:, 1 - j, :, 0, :], sums[:, :, :], h, ALU.add)
                    V.tensor_tensor(uv[:, 1 - j, :, 1, :], sums[:, :, :], h, ALU.mult).then_inc(uv_made, 1)
                    dve.wait_ge(uv_made, t)
                if l == 0:
                    select(t + 1, 1 - j, range(5, CG))
                    if live(t, 2):
                        g = t - 2
                        dve.wait_ge(hi_made, g + 1)
                        done(dve, y_made, g)
                        V.tensor_tensor(rest[:, :, :], yf[:, :, :], y[:, j, :, 0, :], ALU.subtract).then_inc(rest_made, 1)
                else:
                    if live(t, 2):
                        g = t - 2
                        dve.wait_ge(multiplied, g + 1)
                        if final(g):
                            dve.wait_ge(res_in[j], 16 * (GROUPS // 2 + 2))
                        else:
                            moved(dve, res_in[j], g, j)
                        done(dve, y_made, g - 1)
                        V.tensor_tensor(z[:, j], res[:, j], p_out[j][:, :, :], ALU.add).then_inc(z_made, 1)
                    select(t + 1, 1 - j, (5, 6))
                    if live(t, 2):
                        dve.wait_ge(z_made, g + 1)
                        dve.nop(nofuse=True)
                        V.tensor_reduce(total[:, j], z[:, j], AX.X, ALU.add).then_inc(total_made, 1)
                    select(t + 1, 1 - j, (7, 8))
                    if live(t, 2):
                        dve.wait_ge(total_made, g + 1)
                        V.scalar_tensor_tensor(z[:, j], total[:, j].unsqueeze(2).to_broadcast([P, GN, D]), -1.0 / D, z[:, j],
                                               ALU.mult, ALU.add).then_inc(centred, 1)
            steps(dve, body)


GP = 125
G_CHUNKS = N_EDGES // GP
G_TILES = N_NODES // GP
G_GROUP = 8
G_GROUPS = G_TILES // G_GROUP
assert G_CHUNKS * GP == N_EDGES and G_GROUPS * G_GROUP * GP == N_NODES
G_DRAM = {"g_table": (N_NODES, D), "g_hidden": (N_NODES, D), "g_sums": (N_NODES + GP, D),
          "g_deg0": (N_NODES + GP, 1), "g_deg1": (N_NODES + GP, 1)}


def general_path(nc, x, src, dst, weights, out, dram, run_if):
    with ExitStack() as ctx:
        def sb(name, shape, dt=F32):
            return ctx.enter_context(nc.sbuf_tensor("g_" + name, shape, dt))

        def sem(name):
            return ctx.enter_context(nc.semaphore("g_" + name))

        ident, before = sb("ident", [GP, GP]), sb("before", [GP, GP])
        spare_i, spare = sb("spare_i", [GP, 1], I32), sb("spare", [GP, 1])
        ones, zero, eps = sb("ones", [GP, 1]), sb("zero", [GP, G_GROUP * D]), sb("eps", [GP, 1])
        wcat = sb("wcat", [2 * D, 2, D])
        key_i, key, key_b = sb("key_i", [GP, 1], I32), sb("key", [GP, 1]), sb("key_b", [GP, GP])
        from_i = sb("from_i", [GP, 1], I32)
        same, same_before = sb("same", [GP, GP]), sb("same_before", [GP, GP])
        n_before, first, shifted, to_f = (sb(n, [GP, 1]) for n in ("n_before", "first", "shifted", "to_f"))
        to_i = sb("to_i", [GP, 1], I32)
        rows, total = sb("rows", [GP, D]), sb("total", [GP, D])
        deg, root, norm, newton = (sb(n, [GP, 2, G_TILES]) for n in ("deg", "root", "norm", "newton"))
        xg, sg, yg, zg, sq = (sb(n, [GP, G_GROUP, D]) for n in ("xg", "sg", "yg", "zg", "sq"))
        uv, uvt = sb("uv", [GP, G_GROUP, 2, D]), sb("uvt", [P, G_GROUP, GP])
        mean, var, std, rstd = (sb(n, [GP, G_GROUP]) for n in ("mean", "var", "std", "rstd"))
        res = sb("res", [GP, G_GROUP, D])
        p_row = ctx.enter_context(nc.psum_tensor("g_p_row", [GP, 512], F32))
        p_sum = ctx.enter_context(nc.psum_tensor("g_p_sum", [GP, 512], F32))
        p_turn = [ctx.enter_context(nc.psum_tensor(f"g_p_turn{h}", [P, 512], F32)) for h in range(2)]
        p_out = ctx.enter_context(nc.psum_tensor("g_p_out", [GP, 512], F32))

        made, consts, cleared, w_in = sem("made"), sem("consts"), sem("cleared"), sem("w_in")
        key_in, key_spread, key_turned, same_made = sem("key_in"), sem("key_spread"), sem("key_turned"), sem("same_made")
        gathered, summed, total_made, added = sem("gathered"), sem("summed"), sem("total_made"), sem("added")
        deg_in, deg_made, rooted = sem("deg_in"), sem("deg_made"), sem("rooted")
        group_in, sums_in, uv_made, turned, uvt_made = sem("group_in"), sem("sums_in"), sem("uv_made"), sem("turned"), sem("uvt_made")
        multiplied, act_made, centred, squared = sem("multiplied"), sem("act_made"), sem("centred"), sem("squared")
        var_made, std_made, group_made, group_out = sem("var_made"), sem("std_made"), sem("group_made"), sem("group_out")
        hidden_out = sem("hidden_out")
        block = ctx.enter_context(nc.Block())

        by_lane = "(p t) d -> p t d"
        xv, ov = x.rearrange(by_lane, p=GP), out.rearrange(by_lane, p=GP)
        tv, hv = dram["g_table"].rearrange(by_lane, p=GP), dram["g_hidden"].rearrange(by_lane, p=GP)
        sv = dram["g_sums"][0:N_NODES, :].rearrange(by_lane, p=GP)
        PASSES = [(src, dram["g_deg0"], False), (dst, dram["g_deg1"], False),
                  (dst, dram["g_sums"], True), (dst, dram["g_sums"], True)]

        @block.sync
        def _(sp):
            with run_if(sp):
                for l in range(2):
                    for k in range(2):
                        sp.dma_start(wcat[k * D:(k + 1) * D, l, :], weights[2 * l + k]).then_inc(w_in, 16)

                def keys(n):
                    with sp.Fori(0, G_CHUNKS) as c:
                        sp.dma_start(key_i[:, :], PASSES[n][0][bass.ds(c * GP, GP)].unsqueeze(1)).then_inc(key_in, 16)
                        sp.dma_start(from_i[:, :], src[bass.ds(c * GP, GP)].unsqueeze(1)).then_inc(key_in, 16)
                        sp.wait_ge(added, 16 * c + 16 * (1 + n * G_CHUNKS))
                        sp.nop(nofuse=True)

                part = lambda g: bass.ds(g * G_GROUP, G_GROUP)
                keys(0)
                keys(1)
                sp.wait_ge(added, 16 * 2 * G_CHUNKS)
                for k in range(2):
                    sp.dma_start(deg[:, k, :], dram[f"g_deg{k}"][0:N_NODES, :].rearrange("(p t) one -> p (t one)", p=GP)).then_inc(deg_in, 16)
                with sp.Fori(0, G_GROUPS) as g:
                    sp.dma_start(xg[:, :, :], xv[:, part(g), :]).then_inc(group_in, 16)
                    sp.wait_ge(group_made, g + 1)
                    sp.dma_start(tv[:, part(g), :], yg[:, :, :]).then_inc(group_out, 16)
                    sp.wait_ge(group_out, 16 * g + 16)
                    sp.nop(nofuse=True)
                for l in range(2):
                    keys(2 + l)
                    sp.wait_ge(added, 16 * (3 + l) * G_CHUNKS)
                    done = G_GROUPS * (1 + l)
                    with sp.Fori(0, G_GROUPS) as g:
                        sp.dma_start(xg[:, :, :], (xv if l == 0 else hv)[:, part(g), :]).then_inc(group_in, 16)
                        sp.dma_start(res[:, :, :], xv[:, part(g), :]).then_inc(group_in, 16)
                        sp.dma_start(sg[:, :, :], sv[:, part(g), :]).then_inc(group_in, 16)
                        sp.wait_ge(group_made, g + (1 + done))
                        sp.dma_start((tv if l == 0 else ov)[:, part(g), :], yg[:, :, :]).then_inc(group_out, 16)
                        if l == 0:
                            sp.dma_start(hv[:, part(g), :], zg[:, :, :]).then_inc(hidden_out, 16)
                            sp.wait_ge(hidden_out, 16 * g + 16)
                            sp.nop(nofuse=True)
                        sp.wait_ge(group_out, 16 * g + 16 * (1 + done))
                        sp.nop(nofuse=True)

        @block.gpsimd
        def _(pool):
            with run_if(pool):
                nc.gpsimd.memset(ident[:, :], 0.0).then_inc(consts, 1)
                nc.gpsimd.memset(before[:, :], 1.0).then_inc(consts, 1)
                nc.gpsimd.memset(zero[:, :], 0.0).then_inc(consts, 1)
                nc.gpsimd.iota(spare_i[:, :], pattern=[[1, 1]], base=N_NODES, channel_multiplier=1).then_inc(consts, 1)
                pool.wait_ge(consts, 4)
                nc.gpsimd.affine_select(out=ident[:, :], in_=ident[:, :], compare_op=ALU.not_equal, fill=1.0,
                                        base=0, pattern=[[-1, GP]], channel_multiplier=1).then_inc(consts, 1)
                nc.gpsimd.affine_select(out=before[:, :], in_=before[:, :], compare_op=ALU.is_gt, fill=0.0,
                                        base=0, pattern=[[-1, GP]], channel_multiplier=1).then_inc(consts, 1)

                def clear_sums():
                    with pool.Fori(0, G_GROUPS) as g:
                        pool.dma_start(sv[:, bass.ds(g * G_GROUP, G_GROUP), :],
                                       zero[:, :].rearrange("p (t d) -> p t d", d=D)).then_inc(cleared, 16)
                for k in range(2):
                    pool.dma_start(dram[f"g_deg{k}"][0:N_NODES, :].rearrange("(p t) one -> p (t one)", p=GP),
                                   zero[:, 0:G_TILES]).then_inc(cleared, 16)
                    pool.dma_start(dram[f"g_deg{k}"][N_NODES:, :], zero[:, 0:1]).then_inc(cleared, 16)
                clear_sums()
                pool.dma_start(dram["g_sums"][N_NODES:, :], zero[:, 0:D]).then_inc(cleared, 16)
                pool.wait_ge(cleared, 16 * (5 + G_GROUPS))
                for n, (_, into, gather) in enumerate(PASSES):
                    done = n * G_CHUNKS
                    if n == 3:
                        pool.wait_ge(group_in, 16 * 4 * G_GROUPS)
                        clear_sums()
                        pool.wait_ge(cleared, 16 * (5 + 2 * G_GROUPS))
                    with pool.Fori(0, G_CHUNKS) as c:
                        if gather:
                            pool.wait_ge(key_in, 32 * c + 32 * (1 + done))
                            pool.nop(nofuse=True)
                            pool.wait_ge(group_out, 16 * G_GROUPS * (n - 1))
                            pool.indirect_dma_start(out=rows[:, :], out_offset=None, in_=dram["g_table"],
                                                    in_offset=bass.IndirectOffsetOnAxis(ap=from_i[:, :], axis=0)).then_inc(gathered, 16)
                        pool.wait_ge(total_made, c + (1 + done))
                        pool.nop(nofuse=True)
                        pool.indirect_dma_start(out=into, out_offset=bass.IndirectOffsetOnAxis(ap=to_i[:, :], axis=0),
                                                in_=total[:, 0:D if gather else 1], in_offset=None, compute_op=ALU.add).then_inc(added, 16)
                        pool.wait_ge(added, 16 * c + 16 * (1 + done))
                        pool.nop(nofuse=True)

        @block.tensor
        def _(pe):
            with run_if(pe):
                pe.wait_ge(consts, 6)
                pe.wait_ge(w_in, 64)

                def edges(n):
                    done, gather = n * G_CHUNKS, PASSES[n][2]
                    with pe.Fori(0, G_CHUNKS) as c:
                        pe.wait_ge(key_spread, c + (1 + done))
                        nc.tensor.matmul(p_row[:, 0:GP], key_b[:, :], ident[:, :], start=True, stop=True).then_inc(key_turned, 1)
                        pe.wait_ge(same_made, c + (1 + done))
                        if gather:
                            pe.wait_ge(gathered, 16 * c + 16 * (1 + (n - 2) * G_CHUNKS))
                            nc.tensor.matmul(p_sum[:, 0:D], same[:, :], rows[:, :], start=True, stop=True).then_inc(summed, 1)
                        else:
                            nc.tensor.matmul(p_sum[:, 0:1], same[:, :], ones[:, :], start=True, stop=True).then_inc(summed, 1)
                edges(0)
                edges(1)
                for l in range(2):
                    edges(2 + l)
                    with pe.Fori(0, G_GROUPS) as g:
                        pe.wait_ge(uv_made, g + (1 + l * G_GROUPS))
                        for t in range(G_GROUP):
                            last = nc.tensor.transpose(p_turn[t // 4][:, (t % 4) * GP:(t % 4 + 1) * GP],
                                                       uv[:, t].rearrange("p a d -> p (a d)"), ident[:, :])
                        last.then_inc(turned, 1)
                        pe.wait_ge(uvt_made, g + (1 + l * G_GROUPS))
                        for t in range(G_GROUP):
                            last = nc.tensor.matmul(p_out[:, t * D:(t + 1) * D], uvt[:, t, :], wcat[:, l, :], start=True, stop=True)
                        last.then_inc(multiplied, 1)

        @block.scalar
        def _(act):
            with run_if(act):
                act.wait_ge(deg_made, 1)
                nc.scalar.activation(root[:, :, :], deg[:, :, :], ACT.Sqrt).then_inc(rooted, 1)
                for l in range(2):
                    with act.Fori(0, G_GROUPS) as g:
                        act.wait_ge(turned, g + (1 + l * G_GROUPS))
                        nc.scalar.activation(uvt[:, 0:4, :], p_turn[0][:, 0:4 * GP].rearrange("p (t n) -> p t n", n=GP), ACT.Copy)
                        nc.scalar.activation(uvt[:, 4:8, :], p_turn[1][:, 0:4 * GP].rearrange("p (t n) -> p t n", n=GP),
                                             ACT.Copy).then_inc(uvt_made, 1)
                        if l == 1:
                            act.wait_ge(centred, g + 1)
                            nc.scalar.activation(sq[:, :, :], zg[:, :, :], ACT.Square).then_inc(squared, 1)
                            act.wait_ge(var_made, g + 1)
                            nc.scalar.activation(std[:, :], var[:, :], ACT.Sqrt, bias=eps[:, :], scale=1.0 / D).then_inc(std_made, 1)

        @block.vector
        def _(dve):
            with run_if(dve):
                V = nc.vector
                V.memset(ones[:, :], 1.0)
                V.memset(eps[:, :], EPS)
                dve.wait_ge(consts, 6)
                V.tensor_copy(spare[:, :], spare_i[:, :]).then_inc(made, 1)
                dve.wait_ge(made, 1)
                count = [1]

                def stepper(base, per_round, i):
                    n = [0]

                    def step(ins):
                        n[0] += 1
                        ins.then_inc(made, 1)
                        dve.wait_ge(made, i * per_round + (base + n[0]))
                    return step, n

                def edges(n):
                    done, gather = n * G_CHUNKS, PASSES[n][2]
                    K = 8
                    with dve.Fori(0, G_CHUNKS) as c:
                        step, k = stepper(count[0], K, c)
                        dve.wait_ge(key_in, 32 * c + 32 * (1 + done))
                        step(V.tensor_copy(key[:, :], key_i[:, :]))
                        V.tensor_copy(key_b[:, :], key[:, :].to_broadcast([GP, GP])).then_inc(key_spread, 1)
                        step(V.tensor_tensor(shifted[:, :], key[:, :], spare[:, :], ALU.subtract))
                        dve.wait_ge(key_turned, c + (1 + done))
                        step(V.tensor_scalar(same[:, :], p_row[:, 0:GP], key[:, :], None, ALU.is_equal))
                        V.tensor_copy(total[:, 0:1], ones[:, :]).then_inc(same_made, 1)
                        step(V.tensor_tensor(same_before[:, :], same[:, :], before[:, :], ALU.mult))
                        step(V.tensor_reduce(n_before[:, :], same_before[:, :], AX.X, ALU.add))
                        step(V.tensor_scalar(first[:, :], n_before[:, :], 0.0, None, ALU.is_equal))
                        step(V.scalar_tensor_tensor(to_f[:, :], shifted[:, :], first[:, :], spare[:, :], ALU.mult, ALU.add))
                        step(V.tensor_copy(to_i[:, :], to_f[:, :]))
                        dve.wait_ge(summed, c + (1 + done))
                        w = D if gather else 1
                        V.tensor_copy(total[:, 0:w], p_sum[:, 0:w]).then_inc(total_made, 1)
                        assert k[0] == K
                    count[0] += K * G_CHUNKS

                def spread(k, g):
                    return norm[:, k, bass.ds(g * G_GROUP, G_GROUP)].unsqueeze(2).to_broadcast([GP, G_GROUP, D])
                edges(0)
                edges(1)
                dve.wait_ge(deg_in, 32)
                step, k = stepper(count[0], 0, 0)
                step(V.tensor_scalar(deg[:, :, :], deg[:, :, :], 1.0, None, ALU.max))
                V.memset(newton[:, :, :], 0.0).then_inc(deg_made, 1)
                dve.wait_ge(rooted, 1)
                step(V.reciprocal(norm[:, :, :], root[:, :, :]))
                step(V.tensor_tensor(newton[:, :, :], norm[:, :, :], norm[:, :, :], ALU.mult))
                step(V.tensor_tensor(newton[:, :, :], newton[:, :, :], deg[:, :, :], ALU.mult))
                step(V.tensor_scalar(newton[:, :, :], newton[:, :, :], -0.5, 1.5, ALU.mult, ALU.add))
                step(V.tensor_tensor(norm[:, :, :], norm[:, :, :], newton[:, :, :], ALU.mult))
                count[0] += k[0]
                with dve.Fori(0, G_GROUPS) as g:
                    dve.wait_ge(group_in, 16 * g + 16)
                    V.tensor_tensor(yg[:, :, :], xg[:, :, :], spread(0, g), ALU.mult).then_inc(group_made, 1)
                for l in range(2):
                    edges(2 + l)
                    K = 3 if l == 0 else 7
                    with dve.Fori(0, G_GROUPS) as g:
                        step, k = stepper(count[0], K, g)
                        dve.wait_ge(group_in, 48 * g + (48 + 16 * G_GROUPS + 48 * l * G_GROUPS))
                        step(V.tensor_tensor(sg[:, :, :], sg[:, :, :], spread(1, g), ALU.mult))
                        V.tensor_tensor(uv[:, :, 0, :], sg[:, :, :], xg[:, :, :], ALU.add)
                        step(V.tensor_tensor(uv[:, :, 1, :], sg[:, :, :], xg[:, :, :], ALU.mult))
                        V.tensor_copy(mean[:, :], norm[:, 0, 0:G_GROUP]).then_inc(uv_made, 1)
                        dve.wait_ge(multiplied, g + (1 + l * G_GROUPS))
                        product = p_out[:, 0:G_GROUP * D].rearrange("p (t d) -> p t d", d=D)
                        if l == 0:
                            step(V.tensor_scalar(zg[:, :, :], product, 0.0, None, ALU.max))
                            V.tensor_tensor(yg[:, :, :], zg[:, :, :], spread(0, g), ALU.mult).then_inc(group_made, 1)
                        else:
                            across = lambda a: a[:, :].unsqueeze(2).to_broadcast([GP, G_GROUP, D])
                            step(V.tensor_tensor(zg[:, :, :], res[:, :, :], product, ALU.add))
                            step(V.tensor_reduce(mean[:, :], zg[:, :, :], AX.X, ALU.add))
                            step(V.tensor_scalar(mean[:, :], mean[:, :], 1.0 / D, None, ALU.mult))
                            V.tensor_tensor(zg[:, :, :], zg[:, :, :], across(mean), ALU.subtract).then_inc(centred, 1)
                            dve.wait_ge(squared, g + 1)
                            step(V.tensor_reduce(var[:, :], sq[:, :, :], AX.X, ALU.add))
                            V.tensor_copy(mean[:, :], norm[:, 0, 0:G_GROUP]).then_inc(var_made, 1)
                            dve.wait_ge(std_made, g + 1)
                            step(V.reciprocal(rstd[:, :], std[:, :]))
                            V.tensor_tensor(yg[:, :, :], zg[:, :, :], across(rstd), ALU.mult).then_inc(group_made, 1)
                        assert k[0] == K
                    count[0] += K * G_GROUPS


class Kept:

    def __init__(k, keep, ctx, weights):
        k.weights = weights
        k.ident, k.ones, k.eps, k.lane_no = (keep(n, [P, w], F32, ctx) for n, w in (("ident", P), ("ones", 1), ("eps", 1), ("lane_no", 1)))
        k.place, k.place16 = keep("place", [P, 3 * P], F32, ctx), keep("place16", [P, TILES], F16, ctx)
        k.wcat = keep("wcat", [2 * D, 2, D], F32, ctx)
        k.row_i = keep("row_i", [P, CHUNKS], I32, ctx)
        k.rel, k.src_lane, k.src_tile = (keep(n, [P, CHUNKS], F32, ctx) for n in ("rel", "src_lane", "src_tile"))
        k.deg, k.norm, k.norm2 = (keep(n, [P, TILES], F32, ctx) for n in ("deg", "norm", "norm2"))
        k.extreme, k.tally = keep("extreme", [P, 4], F32, ctx), keep("tally", [P, 4], F32, ctx)
        k.lanes = keep("lanes", [P, P, RG], F16, ctx)
        k.lane_r, k.rel_c = keep("lane_r", [P, RAWS], F16, ctx), keep("rel_c", [P, RAWS, 2], F16, ctx)
        k.deg_r, k.parts = keep("deg_r", [P, RAWS], F16, ctx), keep("parts", [P, RAWS, 3], F16, ctx)


INPUTS = ["x", "src", "dst", "L0_gnn_W1_1", "L0_gnn_W2_1", "L0_gnn_W1_2", "L0_gnn_W2_2"]


def build(nc, x, src, dst, weights, out, dram):
    tables = [dram["table0"], dram["table1"]]
    with ExitStack() as last:
        def keep(name, shape, dt=F32, stack=last):
            return stack.enter_context(nc.sbuf_tensor("k_" + name, shape, dt))
        flag = keep("flag", [1, 1], I32)
        with ExitStack() as ctx:
            k = Kept(keep, ctx, weights)
            place_edges(nc, src, dst, k)
            k.xh = keep("xh", [P, TILES, D], F32, ctx)
            sort_edges(nc, x, tables[0], k)
            k.p_count = ctx.enter_context(nc.psum_tensor("k_p_count", [P, 512], F32))
            for l in range(2):
                layer(nc, l, x, out, tables, flag, k)

        def if_needed(eng):
            return eng.If(eng.value_load(flag[0:1, 0:1]) > 0)
        general_path(nc, x, src, dst, weights, out, dram, if_needed)


def kernel(**inputs):
    import concourse.bacc as bacc
    from concourse.bass_utils import run_bass_kernel_spmd

    nc = bacc.Bacc("TRN2", target_bir_lowering=False, num_devices=1)
    arrays, aps = {}, {}
    for name in INPUTS:
        a = np.ascontiguousarray(inputs[name])
        arrays["in_" + name] = a
        aps[name] = nc.dram_tensor("in_" + name, a.shape, mybir.dt.from_np(a.dtype), kind="ExternalInput").ap()
    out = nc.dram_tensor("out", (N_NODES, D), F32, kind="ExternalOutput").ap()
    dram = {n: nc.dram_tensor(n, s, F32, kind="Internal").ap() for n, s in dict(G_DRAM, table0=(P, TILES * D)).items()}
    dram["table1"] = nc.dram_tensor("table1", (P, TILES * PARTS * D), BF16, kind="Internal").ap()
    build(nc, aps["x"], aps["src"], aps["dst"], [aps[n] for n in INPUTS[3:]], out, dram)
    r = run_bass_kernel_spmd(nc, [arrays], core_ids=[0])
    return r.results[0]["out"]
```
